# Optimizing a Trainium2 kernel written in Bass

```python
import numpy as np
import jax
import jax.numpy as jnp

def _softmax(x, axis=-1):
    return jax.nn.softmax(x, axis=axis)
def _gelu(x):
    return jax.nn.gelu(x, approximate=True)
def _silu(x):
    return jax.nn.silu(x)
def _sigmoid(x):
    return jax.nn.sigmoid(x)
def _layernorm(x, axis=-1, eps=1e-5):
    m = jnp.mean(x, axis=axis, keepdims=True)
    v = jnp.var(x, axis=axis, keepdims=True)
    return (x - m) / jnp.sqrt(v + eps)
def _scatter_add(tgt, idx, src, axis=0):
    return tgt.at[idx].add(src)
def _segment_sum(src, seg, n):
    return jax.ops.segment_sum(src, seg, n)

kernel_name = 'mk_conv_seq_d2_conv_nchw256_7ca1c2'

def setup_inputs(seed: int = 0):
    np.random.seed(seed)
    _w = jnp.asarray
    def _rec_inputs():
        import jax
        import jax.numpy as jnp
        _gk = jax.random.key(seed)
        x = -0.0002928 + 1 * jax.random.normal(jax.random.fold_in(_gk, 1), (4, 256, 64, 64), jnp.float32)
        return x
    x = _rec_inputs()
    def _L0_conv_setup():
        import jax, jax.numpy as jnp
        import numpy as np
        key = jax.random.key(seed)
        k1, k2, k3 = jax.random.split(key, 3)
        B, C, H, W = (4, 256, 64, 64)
        K = max(C // 16, 8)
        x = jax.random.normal(k1, (B, C, H, W), dtype=jnp.float32)
        w1 = jax.random.normal(k2, (K, C), dtype=jnp.float32) * (1.0 / np.sqrt(C))
        b1 = jax.random.normal(k3, (K,), dtype=jnp.float32) * 0.01
        return {'x': x, 'w1': w1, 'b1': b1}
    _L0_conv_all = _L0_conv_setup()
    _L0_conv_in = {k: v for k, v in _L0_conv_all.items() if k in ('w1', 'b1', )}
    del _L0_conv_all

    def _L1_conv_setup():
        import jax, jax.numpy as jnp
        import numpy as np
        EPS = 1e-05

        def _binary_act(x):
            sgn = jnp.sign(x)
            ax = jnp.clip(x, -1.0, 1.0)
            out3 = jnp.where(ax < 0, ax * ax + 2.0 * ax, -ax * ax + 2.0 * ax)
            return jax.lax.stop_gradient(sgn - out3) + out3

        def _binarize_weights(w):
            alpha = jax.lax.stop_gradient(jnp.mean(jnp.abs(w), axis=(1, 2, 3), keepdims=True))
            cw = jnp.clip(w, -1.0, 1.0)
            return jax.lax.stop_gradient(alpha * jnp.sign(w) - cw) + cw

        def _block(x, weights, gamma, beta):
            a = _binary_act(x)
            bw = _binarize_weights(weights)
            y = jax.lax.conv_general_dilated(a, bw, window_strides=(1, 1), padding=((1, 1), (1, 1)), dimension_numbers=('NCHW', 'OIHW', 'NCHW'))
            mu = jnp.mean(y, axis=(0, 2, 3), keepdims=True)
            var = jnp.mean((y - mu) ** 2, axis=(0, 2, 3), keepdims=True)
            yhat = (y - mu) * jax.lax.rsqrt(var + EPS)
            out = yhat * gamma[None, :, None, None] + beta[None, :, None, None]
            return out + x
        key = jax.random.key(seed)
        k1, k2 = jax.random.split(key)
        N, C, H, W = (32, 256, 56, 56)
        x = jax.random.normal(k1, (N, C, H, W), dtype=jnp.float32)
        weights = jax.random.normal(k2, (C, C, 3, 3), dtype=jnp.float32) * 0.001
        gamma = jnp.ones((C,), dtype=jnp.float32)
        beta = jnp.zeros((C,), dtype=jnp.float32)
        return {'x': x, 'weights': weights, 'gamma': gamma, 'beta': beta}
    _L1_conv_all = _L1_conv_setup()
    _L1_conv_in = {k: v for k, v in _L1_conv_all.items() if k in ('weights', 'gamma', 'beta', )}
    del _L1_conv_all

    return {
        "x": x,
        "L0_conv_w1": _L0_conv_in["w1"],
        "L0_conv_b1": _L0_conv_in["b1"],
        "L1_conv_weights": _L1_conv_in["weights"],
        "L1_conv_gamma": _L1_conv_in["gamma"],
        "L1_conv_beta": _L1_conv_in["beta"],
    }

def reference(x, L0_conv_w1, L0_conv_b1, L1_conv_weights, L1_conv_gamma, L1_conv_beta):
    import jax
    import jax.numpy as jnp
    def _L0_conv_ref(x, w1, b1):
        import jax, jax.numpy as jnp
        import numpy as np
        B, C, H, W = x.shape
        N = H * W
        xf = x.reshape(B, C, N)
        f = jnp.einsum('kc,bcn->bkn', w1, xf) + b1[None, :, None]
        energy = jnp.einsum('bkn,bkm->bnm', f, f)
        attention = jax.nn.softmax(energy, axis=-1)
        out = jnp.einsum('bcm,bnm->bcn', xf, attention)
        out = out.reshape(B, C, H, W)
        return x + out * 0.1

    def _L1_conv_ref(x, weights, gamma, beta):
        import jax, jax.numpy as jnp
        import numpy as np
        EPS = 1e-05

        def _binary_act(x):
            sgn = jnp.sign(x)
            ax = jnp.clip(x, -1.0, 1.0)
            out3 = jnp.where(ax < 0, ax * ax + 2.0 * ax, -ax * ax + 2.0 * ax)
            return jax.lax.stop_gradient(sgn - out3) + out3

        def _binarize_weights(w):
            alpha = jax.lax.stop_gradient(jnp.mean(jnp.abs(w), axis=(1, 2, 3), keepdims=True))
            cw = jnp.clip(w, -1.0, 1.0)
            return jax.lax.stop_gradient(alpha * jnp.sign(w) - cw) + cw

        def _block(x, weights, gamma, beta):
            a = _binary_act(x)
            bw = _binarize_weights(weights)
            y = jax.lax.conv_general_dilated(a, bw, window_strides=(1, 1), padding=((1, 1), (1, 1)), dimension_numbers=('NCHW', 'OIHW', 'NCHW'))
            mu = jnp.mean(y, axis=(0, 2, 3), keepdims=True)
            var = jnp.mean((y - mu) ** 2, axis=(0, 2, 3), keepdims=True)
            yhat = (y - mu) * jax.lax.rsqrt(var + EPS)
            out = yhat * gamma[None, :, None, None] + beta[None, :, None, None]
            return out + x
        return _block(x, weights, gamma, beta)

    def _gn(v, G=32, eps=1e-5):
        B_, C_, H_, W_ = v.shape
        g = v.reshape(B_, G, C_ // G, H_, W_)
        m = jnp.mean(g, axis=(2, 3, 4), keepdims=True)
        s = jnp.var(g, axis=(2, 3, 4), keepdims=True)
        return ((g - m) / jnp.sqrt(s + eps)).reshape(v.shape)

    def _ln_c(v, eps=1e-6):
        m = jnp.mean(v, axis=1, keepdims=True)
        s = jnp.var(v, axis=1, keepdims=True)
        return (v - m) / jnp.sqrt(s + eps)

    def _ln_t(v, eps=1e-5):
        m = jnp.mean(v, axis=-1, keepdims=True)
        s = jnp.var(v, axis=-1, keepdims=True)
        return (v - m) / jnp.sqrt(s + eps)

    def _to_tokens(v):
        B_, C_, H_, W_ = v.shape
        return v.reshape(B_, C_, H_ * W_).transpose(0, 2, 1)
    def _from_tokens(t, like):
        B_, C_, H_, W_ = like.shape
        return t.transpose(0, 2, 1).reshape(B_, C_, H_, W_)

    x = _L0_conv_ref(x, L0_conv_w1, L0_conv_b1)
    x = _L1_conv_ref(x, L1_conv_weights, L1_conv_gamma, L1_conv_beta)
    return x


_drawn_inputs = setup_inputs


def setup_inputs(seed=0):
    import zlib

    import numpy as np

    out = dict(_drawn_inputs(seed))
    spreads = {'L1_conv_gamma': (1.0, 0.2), 'L1_conv_beta': (0.0, 0.1)}
    factors = {'L0_conv_b1': 3.862}
    for name, (base, spread) in spreads.items():
        noise = np.random.default_rng([zlib.crc32(name.encode()), seed]).standard_normal(out[name].shape)
        drawn = base * np.exp(spread * noise) if base else spread * noise
        out[name] = jnp.asarray(drawn.astype(out[name].dtype))
    for name, factor in factors.items():
        out[name] = (out[name] * factor).astype(out[name].dtype)
    return out
```

```python
from contextlib import ExitStack

import numpy as np
import concourse.bass as bass
from concourse import mybir

F32 = mybir.dt.float32
F32R = mybir.dt.float32r
BF16 = mybir.dt.bfloat16
I16 = mybir.dt.int16
ALU = mybir.AluOpType
ACT = mybir.ActivationFunctionType
AX = mybir.AxisListType
ds = bass.ds

NB, C, H, W = 4, 256, 64, 64
N = H * W
CT = C // 128
KF = 16
SPLIT_A = (1, 1, 2, 2, 1, 3)
SPLIT_B = (1, 2, 1, 2, 3, 1)
KE = KF * len(SPLIT_A)
KS = KE + 3
MT = N // 128
QC = 256
QT = QC // 128
CH = N // QC
GM = 4
G = MT // GM
RP = 4
SC = 512
SCN = QT * N // SC
SL = N // 512
XQ = 4
DEN = 10.0
EPS = 1e-5
TAPS = 9
PW = W + 2
RC = 8
NRC = H // RC


def items_of(parts):
    out = []
    for g in range(G):
        if "spread" in parts and g < G - 1:
            out += [(g, "xt", 0), (g, "xt", 1)]
        if "border" in parts and g == G - 1:
            out += [(g, "xt", 0), (g, "xt", 1)]
        if g == 1 and "last" not in parts:
            out += [(g, "shift", 0)]
        if g == 1:
            out += [(g, "back", 0)]
        if "project" in parts and g in (2, 5):
            out += [(g, "project", 0)]
        if "scan" in parts:
            out += [(g, "scan", 0), (g, "scan", 1)]
    return {(g, kind, k): n % 2 for n, (g, kind, k) in enumerate(out)}


def walk(eng, chunk):
    with eng.Fori(0, NB - 1) as b:
        chunk(b, 0, ("scan", "spread"))
        with eng.Fori(1, 3) as j:
            chunk(b, j, ("scan",))
        with eng.Fori(3, 3 + SL // 2) as j:
            chunk(b, j, ("scan", "project"))
        with eng.Fori(3 + SL // 2, CH - 2) as j:
            chunk(b, j, ("scan",))
        chunk(b, CH - 2, ("scan", "scan_next"))
        chunk(b, CH - 1, ("scan", "scan_next", "border"))
    chunk(NB - 1, 0, ("scan", "spread"))
    with eng.Fori(1, CH - 2) as j:
        chunk(NB - 1, j, ("scan",))
    chunk(NB - 1, CH - 2, ())
    chunk(NB - 1, CH - 1, ("last",))


def attention(nc, x, w1r, cols, ident, x2d):
    with ExitStack() as ctx:
        def sb(name, shape, dt):
            return ctx.enter_context(nc.sbuf_tensor(name, shape, dt))

        def ps(name, shape, dt=F32):
            return ctx.enter_context(nc.psum_tensor(name, shape, dt))

        def sem(name):
            return ctx.enter_context(nc.semaphore(name))

        xn = sb("xn", [128, CT, N], F32)
        xh = sb("xh", [128, MT, C + 2], F32R)
        xl = sb("xl", [128, MT, C], F32R)
        A = sb("A", [128, N], BF16)
        Bq = sb("Bq", [128, N], BF16)
        An = sb("An", [128, N], BF16)
        Bn = sb("Bn", [128, N], BF16)
        P = sb("P", [128, 2, GM * QC], F32)
        Ph = sb("Ph", [128, RP, GM, QC], F32R)
        Pl = sb("Pl", [128, RP, GM, QC], F32R)
        w1s = sb("w1s", [128, CT, 128], F32)
        col = sb("col", [128, 8], F32)
        idf = sb("idf", [128, 128], F32)
        idb = sb("idb", [128, 128], BF16)
        Fp = sb("Fp", [128, 512], F32)
        f1 = sb("f1", [128, 512], BF16)
        f2 = sb("f2", [128, 512], BF16)
        ta = sb("ta", [128, 512], F32)
        tb = sb("tb", [128, 512], F32)
        pm = sb("pm", [128, SCN], F32)
        negm = sb("negm", [128, QT], F32)
        ms = sb("ms", [128, 3 * QT], BF16)
        mr = sb("mr", [128, 2, QT], F32)
        mrow = sb("mrow", [3 * QT, 128], BF16)
        rd = sb("rd", [128, QT], F32)
        xs = sb("xs", [128, QT, C], F32)
        x2t = sb("x2t", [128, QT, C], F32)
        x2s = sb("x2s", [128, CT, QC], F32)

        pe2 = [ps(f"pe2_{k}", [128, GM * QC]) for k in range(2)]
        acc = [ps(f"acc_{i}", [128, 512]) for i in range(QT)]
        misc = [ps(f"misc_{k}", [128, 512]) for k in range(2)]

        const_in = sem("const_in")
        idb_done = sem("idb_done")
        fill_done = sem("fill_done")
        x_in = [sem(f"x_in{k}") for k in range(XQ)]
        f_filled = sem("f_filled")
        f_copied = sem("f_copied")
        split_step = sem("split_step")
        ab_done = sem("ab_done")
        border_done = sem("border_done")
        scan_filled = sem("scan_filled")
        scan_reduced = sem("scan_reduced")
        neg_done = sem("neg_done")
        ms_step = sem("ms_step")
        ms_done = sem("ms_done")
        m_filled = sem("m_filled")
        m_copied = sem("m_copied")
        m_stored = sem("m_stored")
        xt_filled = sem("xt_filled")
        xh_done = sem("xh_done")
        xl_done = sem("xl_done")
        e_done = sem("e_done")
        ph_done = sem("ph_done")
        pl_done = sem("pl_done")
        av_done = sem("av_done")
        acc_done = sem("acc_done")
        rd_done = sem("rd_done")
        evac_done = sem("evac_done")
        xs_done = sem("xs_done")
        back_filled = sem("back_filled")
        back_copied = sem("back_copied")
        x2_stored = sem("x2_stored")

        block = ctx.enter_context(nc.Block())

        @block.sync
        def _(sp):
            sp.dma_start(w1s[:], w1r.rearrange("(t p) k -> p t k", p=128)).then_inc(const_in, 16)
            sp.dma_start(col[:], cols).then_inc(const_in, 16)
            sp.dma_start(idf[:], ident).then_inc(const_in, 16)

            def load_x(at):
                batch = x[ds(at, C * N)].rearrange("(t p n) -> p t n", p=128, n=N)
                for k in range(XQ):
                    sp.dma_start(xn[:, :, k * (N // XQ):(k + 1) * (N // XQ)],
                                 batch[:, :, k * (N // XQ):(k + 1) * (N // XQ)]).then_inc(x_in[k], 16)

            def store_shift(due, dst):
                sp.wait_ge(m_copied, due)
                sp.dma_start(dst, mrow[:, :]).then_inc(m_stored, 16)

            def store_x2(due, at):
                sp.wait_ge(back_copied, due)
                sp.dma_start(x2d[ds(at, C * QC)].rearrange("(p n) -> p n", p=128),
                             x2s[:, :, :].rearrange("p c n -> p (c n)")).then_inc(x2_stored, 16)

            load_x(0)
            store_shift(1, Bn[KE:KS, 0:QC].rearrange("k (i c) -> k i c", i=QT))

            def ahead(value):
                return value if isinstance(value, int) else sp.snap(value)

            def chunk(b, j, parts):
                t = b * CH + j
                shift_due, back_due, x2_at = ahead(t + 2), ahead(t + 1), ahead(t * (C * QC))
                if "border" in parts:
                    dst = Bn[KE:KS, 0:QC]
                else:
                    dst = Bq[KE:KS, ds(ahead((j + 1) * QC), QC)] if "last" not in parts else None
                if "spread" in parts and not isinstance(b, int):
                    spread_due, x_at = ahead((b + 1) * (MT // 2)), ahead((b + 1) * (C * N))
                if "last" not in parts:
                    store_shift(shift_due, dst.rearrange("k (i c) -> k i c", i=QT))
                store_x2(back_due, x2_at)
                if "spread" in parts and not isinstance(b, int):
                    sp.wait_ge(xt_filled, spread_due)
                    load_x(x_at)

            walk(sp, chunk)
            store_x2(NB * CH + 1, NB * CH * C * QC)
            sp.wait_ge(x2_stored, 16 * (NB * CH + 1) + 1)

        @block.tensor
        def _(pe):
            pe.wait_ge(const_in, 48)
            pe.wait_ge(idb_done, 1)
            held = {0: None, 1: None}

            def take(bank):
                if held[bank]:
                    pe.wait_ge(*held[bank])

            def project(s, sl, bank, b=None):
                if isinstance(sl, int):
                    pe.wait_ge(x_in[sl * XQ // SL], 16)
                take(bank)
                for c in range(CT):
                    mm = pe.matmul(misc[bank][:], w1s[:, c, :], xn[:, c, ds(sl * 512, 512)],
                                   start=c == 0, stop=c == CT - 1)
                mm.then_inc(f_filled, 1)
                held[bank] = (f_copied, s + 1)

            def scan(T, i, q0, bank, a, bq):
                take(bank)
                mc = i % (N // SC)
                pe.matmul(misc[bank][:], a[0:KE, ds(q0 + (i // (N // SC)) * 128, 128)],
                          bq[0:KE, mc * SC:(mc + 1) * SC], start=True, stop=True).then_inc(scan_filled, 1)
                held[bank] = (scan_reduced, T * SCN + i + 1)

            def shift(T, bank):
                pe.wait_ge(ms_done, T + 1)
                take(bank)
                pe.transpose(misc[bank][0:3 * QT, 0:64].bitcast(BF16), ms[:, :], idb[:, :]).then_inc(m_filled, 1)
                held[bank] = (m_copied, T + 1)

            def back(t, bank):
                pe.wait_ge(evac_done, t * 2 + 2)
                take(bank)
                for c in range(CT):
                    for i in range(QT):
                        mm = pe.transpose(misc[bank][:, c * QC + i * 128:c * QC + (i + 1) * 128],
                                          x2t[:, i, c * 128:(c + 1) * 128], idf[:, :])
                mm.then_inc(back_filled, 1)
                held[bank] = (back_copied, t + 1)

            def spread(b, k, bank):
                take(bank)
                for h in range(2):
                    for c in range(CT):
                        m = 2 * k + h
                        mm = pe.transpose(misc[bank][:, h * C + c * 128:h * C + (c + 1) * 128],
                                          xn[:, c, m * 128:(m + 1) * 128], idf[:, :])
                mm.then_inc(xt_filled, 1)
                held[bank] = (xl_done, b * (MT // 2) + k + 1)

            def energy(g, c0):
                for k in range(GM):
                    m = g * GM + k
                    mm = pe.matmul(pe2[g % 2][:, k * QC:(k + 1) * QC], A[0:KS, m * 128:(m + 1) * 128],
                                   Bq[0:KS, ds(c0, QC)], start=True, stop=True)
                mm.then_inc(e_done, 1)

            def attend(t, g):
                pe.wait_ge(pl_done, t * G + (g + 1))
                for i in range(QT):
                    if g == 0:
                        pe.wait_ge(evac_done, t * 2 + (i + 1))
                    for k in range(GM):
                        m = g * GM + k
                        first, last = g == 0 and k == 0, g == G - 1 and k == GM - 1
                        ph = Ph[:, g % RP, k, i * 128:(i + 1) * 128]
                        pl = Pl[:, g % RP, k, i * 128:(i + 1) * 128]
                        pe.matmul(acc[i][:, 0:C + 2], ph, xh[:, m, :], start=first, stop=False)
                        pe.matmul(acc[i][:, 0:C], ph, xl[:, m, :], start=False, stop=False)
                        mm = pe.matmul(acc[i][:, 0:C + 2], pl, xh[:, m, :], start=False, stop=last)
                        if last and i < QT - 1:
                            mm.then_inc(acc_done, 1)
                        if k == GM - 1 and i == QT - 1:
                            mm.then_inc(av_done, 1)

            for s in range(SL):
                project(s, s, (s + 1) % 2)
            pe.wait_ge(ab_done, 2 * SL)
            for i in range(SCN):
                scan(0, i, 0, (i + 1) % 2, An, Bn)
            shift(0, 1)
            pe.wait_ge(fill_done, 1)
            spread(0, 0, 0)
            spread(0, 1, 1)
            for i in range(SCN):
                scan(1, i, QC, i % 2, An, Bn)
            pe.wait_ge(border_done, 2)
            energy(0, 0)
            energy(1, 0)

            def chunk(b, j, parts):
                t = b * CH + j
                bank = items_of(parts)
                if "last" in parts:
                    held[0], held[1] = (m_copied, t + 1), (back_copied, t)
                else:
                    for k in range(2):
                        held[k] = (scan_reduced, (t + 1) * SCN + (SCN - 1 + k))
                for g in range(G):
                    if "last" not in parts or g < G - 2:
                        pe.wait_ge(ph_done, t * G + (g + 1))
                        if g < G - 2:
                            energy(g + 2, j * QC)
                        else:
                            if g == G - 2:
                                pe.wait_ge(m_stored, (t + 2) * 16)
                            if "border" in parts and g == G - 2:
                                pe.wait_ge(border_done, (b + 2) * 2)
                            energy(g + 2 - G, 0 if "border" in parts else (j + 1) * QC)
                    for (g_, kind, k), bk in bank.items():
                        if g_ != g:
                            continue
                        if kind == "xt":
                            if "border" in parts:
                                for q in range(XQ):
                                    pe.wait_ge(x_in[q], (b + 2) * 16)
                                spread(b + 1, k, bk)
                            else:
                                spread(b, 2 * (g + 1) + k, bk)
                        elif kind == "shift":
                            shift(t + 1, bk)
                        elif kind == "back":
                            back(t, bk)
                        elif kind == "project":
                            sl = (j - 3) * 2 + (0 if g == 2 else 1)
                            for q in range(XQ):
                                pe.wait_ge(x_in[q], (b + 2) * 16)
                            project((b + 1) * SL + sl, sl, bk)
                        elif "scan_next" in parts:
                            scan(t + 2, 2 * g + k, (j - (CH - 2)) * QC, bk, An, Bn)
                        else:
                            scan(t + 2, 2 * g + k, (j + 2) * QC, bk, A, Bq)
                    if "spread" in parts:
                        pe.wait_ge(xl_done, b * (MT // 2) + 2 * (g + 1))
                    attend(t, g)

            walk(pe, chunk)
            held[0], held[1] = (back_copied, NB * CH), None
            back(NB * CH, 0)

        @block.scalar
        def _(act):
            def exps(q, g):
                act.wait_ge(e_done, q + 1)
                if not (isinstance(q, int) and q < 2):
                    act.wait_ge(pl_done, q - 1)
                nc.scalar.activation(P[:, g % 2, :], pe2[g % 2][:], ACT.Exp)
                if not (isinstance(q, int) and q < 2):
                    act.wait_ge(av_done, q - 1)
                nc.scalar.activation(Ph[:, g % RP, :, :].rearrange("p k n -> p (k n)"), pe2[g % 2][:],
                                     ACT.Exp).then_inc(ph_done, 1)

            def project(s, bank):
                act.wait_ge(f_filled, s + 1)
                act.wait_ge(ab_done, s * 2)
                nc.scalar.activation(Fp[0:KS, :], misc[bank][0:KS, :], ACT.Identity,
                                     bias=col[0:KS, 0:1]).then_inc(f_copied, 1)

            def spread(b, k, bank, seen):
                act.wait_ge(xt_filled, b * (MT // 2) + k + 1)
                act.wait_ge(xs_done, seen + 1)
                nc.scalar.copy(xh[:, 2 * k:2 * k + 2, 0:C],
                               misc[bank][:].rearrange("p (m c) -> p m c", m=2)).then_inc(xh_done, 1)

            def back(t, bank):
                act.wait_ge(back_filled, t + 1)
                act.wait_ge(x2_stored, t * 16 + 1)
                nc.scalar.copy(x2s[:, :, :].rearrange("p c n -> p (c n)"), misc[bank][:]).then_inc(back_copied, 1)

            act.wait_ge(const_in, 48)
            for s in range(SL):
                project(s, (s + 1) % 2)
            for k in range(2):
                spread(0, k, k, 0)
            for g in range(2):
                exps(g, g)

            def chunk(b, j, parts):
                t = b * CH + j
                bank = items_of(parts)
                for g in range(G):
                    if "last" not in parts or g < G - 2:
                        exps(t * G + (g + 2), (g + 2) % G)
                    for (g_, kind, k), bk in bank.items():
                        if g_ != g:
                            continue
                        if kind == "xt":
                            if "border" in parts:
                                spread(b + 1, k, bk, b * CH + 2)
                            else:
                                spread(b, 2 * (g + 1) + k, bk, b * CH)
                        elif kind == "back":
                            back(t, bk)
                        elif kind == "project":
                            project((b + 1) * SL + ((j - 3) * 2 + (0 if g == 2 else 1)), bk)

            walk(act, chunk)
            back(NB * CH, 0)

        @block.vector
        def _(dve):
            dve.wait_ge(const_in, 48)
            nc.vector.memset(x2t[:], 0.0).then_inc(evac_done, 2)
            nc.vector.tensor_copy(idb[:], idf[:]).then_inc(idb_done, 1)

            def split(s, sl):
                dve.wait_ge(f_copied, s + 1)
                nc.vector.tensor_copy(f1[0:KS, :], Fp[0:KS, :]).then_inc(split_step, 1)
                dve.wait_ge(split_step, s * 4 + 1)
                nc.vector.scalar_tensor_tensor(f2[0:KS, :], f1[0:KS, :], -1.0, Fp[0:KS, :],
                                               ALU.mult, ALU.add).then_inc(split_step, 1)
                nc.vector.scalar_tensor_tensor(ta[0:KS, :], f1[0:KS, :], col[0:KS, 1:2], Fp[0:KS, :],
                                               ALU.mult, ALU.add).then_inc(split_step, 1)
                nc.vector.scalar_tensor_tensor(tb[0:KS, :], f1[0:KS, :], col[0:KS, 3:4], Fp[0:KS, :],
                                               ALU.mult, ALU.add).then_inc(split_step, 1)
                dve.wait_ge(split_step, s * 4 + 4)
                nc.vector.scalar_tensor_tensor(An[0:KS, ds(sl * 512, 512)], f2[0:KS, :], col[0:KS, 2:3],
                                               ta[0:KS, :], ALU.mult, ALU.add).then_inc(ab_done, 1)
                nc.vector.scalar_tensor_tensor(Bn[0:KS, ds(sl * 512, 512)], f2[0:KS, :], col[0:KS, 4:5],
                                               tb[0:KS, :], ALU.mult, ALU.add).then_inc(ab_done, 1)

            def scan(T, i, bank):
                dve.wait_ge(scan_filled, T * SCN + (i + 1))
                nc.vector.tensor_reduce(pm[:, i:i + 1], misc[bank][:], AX.X, ALU.max).then_inc(scan_reduced, 1)
                per = N // SC
                if i % per == per - 1:
                    h = i // per
                    dve.wait_ge(scan_reduced, T * SCN + (i + 1))
                    dve.wait_ge(ms_done, T)
                    nc.vector.tensor_reduce(negm[:, h:h + 1], pm[:, h * per:(h + 1) * per], AX.X, ALU.max,
                                            negate=True).then_inc(neg_done, 1)

            def shift(T, bank):
                dve.wait_ge(m_filled, T + 1)
                dve.wait_ge(m_stored, T * 16)
                nc.vector.tensor_copy(mrow[:, :], misc[bank][0:3 * QT, 0:64].bitcast(BF16)).then_inc(m_copied, 1)

            def border(b, t):
                dve.wait_ge(ab_done, (b + 1) * (2 * SL))
                dve.wait_ge(m_stored, (t + 1) * 16)
                nc.vector.tensor_copy(A[0:KS, :], An[0:KS, :]).then_inc(border_done, 1)
                nc.vector.tensor_copy(Bq[0:KS, :], Bn[0:KS, :]).then_inc(border_done, 1)

            def spread(b, k, bank):
                dve.wait_ge(xh_done, b * (MT // 2) + k + 1)
                nc.vector.tensor_tensor(xl[:, 2 * k:2 * k + 2, :], misc[bank][:].rearrange("p (m c) -> p m c", m=2),
                                        xh[:, 2 * k:2 * k + 2, 0:C].bitcast(F32), ALU.subtract).then_inc(xl_done, 1)

            def lower(q, g):
                dve.wait_ge(ph_done, q + 1)
                nc.vector.tensor_tensor(Pl[:, g % RP, :, :].rearrange("p k n -> p (k n)"), P[:, g % 2, :],
                                        Ph[:, g % RP, :, :].rearrange("p k n -> p (k n)").bitcast(F32),
                                        ALU.subtract).then_inc(pl_done, 1)

            def evacuate(t, i):
                if i < QT - 1:
                    dve.wait_ge(acc_done, t + 1)
                else:
                    dve.wait_ge(av_done, t * G + (G + 2))
                nc.vector.reciprocal(rd[:, i:i + 1], acc[i][:, C:C + 1]).then_inc(rd_done, 1)
                dve.wait_ge(rd_done, t * 2 + (i + 1))
                dve.wait_ge(xs_done, t + 2)
                dve.wait_ge(back_filled, t + 1)
                nc.vector.scalar_tensor_tensor(x2t[:, i, :], acc[i][:, 0:C], rd[:, i:i + 1], xs[:, i, :],
                                               ALU.mult, ALU.add).then_inc(evac_done, 1)

            for s in range(SL):
                split(s, s)
            for i in range(SCN):
                scan(0, i, (i + 1) % 2)
            shift(0, 1)
            for k in range(2):
                spread(0, k, k)
            border(0, 0)
            for i in range(SCN):
                scan(1, i, i % 2)
            lower(0, 0)

            def chunk(b, j, parts):
                t = b * CH + j
                bank = items_of(parts)
                for g in range(G):
                    for (g_, kind, k), bk in bank.items():
                        if g_ != g:
                            continue
                        if kind == "xt":
                            if "border" in parts:
                                spread(b + 1, k, bk)
                            else:
                                spread(b, 2 * (g + 1) + k, bk)
                        elif kind == "shift":
                            shift(t + 1, bk)
                        elif kind == "scan":
                            scan(t + 2, 2 * g + k, bk)
                    if "project" in parts and g in (3, 6):
                        sl = (j - 3) * 2 + (0 if g == 3 else 1)
                        split((b + 1) * SL + sl, sl)
                    if "last" not in parts or g < G - 1:
                        lower(t * G + (g + 1), (g + 1) % G)
                    if "border" in parts and g == G - 3:
                        dve.wait_ge(e_done, (t + 1) * G)
                        border(b + 1, t + 1)
                    if g == G - 1:
                        for i in range(QT):
                            evacuate(t, i)

            walk(dve, chunk)

        @block.gpsimd
        def _(pool):
            nc.gpsimd.memset(xh[:, :, C:C + 2].bitcast(F32), DEN).then_inc(fill_done, 1)
            pool.wait_ge(fill_done, 1)
            nc.gpsimd.memset(mr[:], 0.0).then_inc(av_done, 2)
            nc.gpsimd.memset(xs[:], 0.0).then_inc(xs_done, 1)
            nc.gpsimd.memset(x2s[:], 0.0).then_inc(x2_stored, 1)

            pool.wait_ge(av_done, 2)

            def parts_of_max(T):
                pool.wait_ge(neg_done, T * QT + QT)
                pool.wait_ge(m_filled, T)
                nc.gpsimd.tensor_tensor(ms[:, 0:QT], negm[:], mr[:, 1, :], ALU.add).then_inc(ms_step, 1)
                pool.wait_ge(ms_step, T * 3 + 1)
                nc.gpsimd.tensor_tensor(mr[:, 0, :], negm[:], ms[:, 0:QT], ALU.subtract).then_inc(ms_step, 1)
                pool.wait_ge(ms_step, T * 3 + 2)
                nc.gpsimd.tensor_tensor(ms[:, QT:2 * QT], mr[:, 0, :], mr[:, 1, :], ALU.add).then_inc(ms_step, 1)
                pool.wait_ge(ms_step, T * 3 + 3)
                nc.gpsimd.tensor_tensor(ms[:, 2 * QT:3 * QT], mr[:, 0, :], ms[:, QT:2 * QT],
                                        ALU.subtract).then_inc(ms_done, 1)

            parts_of_max(0)

            def chunk(b, j, parts):
                t = b * CH + j
                if "last" not in parts:
                    parts_of_max(t + 1)
                pool.wait_ge(evac_done, t * 2 + 2)
                if "spread" in parts:
                    pool.wait_ge(xl_done, b * (MT // 2) + 2)
                else:
                    pool.wait_ge(xl_done, (b + 1) * (MT // 2))
                nc.gpsimd.tensor_tensor(xs[:], xh[:, ds(j * QT, QT), 0:C].bitcast(F32),
                                        xl[:, ds(j * QT, QT), :].bitcast(F32), ALU.add).then_inc(xs_done, 1)

            walk(pool, chunk)


def convolution(nc, wn, wt, gb, x2d, out):
    SLOT = (0, 1, 2, 0)
    LAST = (1, 2, 3, 0)
    PIECE = N // 4
    HH = H // 2
    with ExitStack() as ctx:
        def sb(name, shape, dt):
            return ctx.enter_context(nc.sbuf_tensor(name, shape, dt))

        def sem(name):
            return ctx.enter_context(nc.semaphore(name))

        xr = [sb(f"xr{k}", [128, CT, N], F32) for k in range(3)]
        Y = sb("Y", [128, CT, NB, N], I16)
        pad = sb("pad", [128, 2, CT, HH + 2, PW], BF16)
        ws = sb("ws", [128, CT, TAPS, C], BF16)
        z = sb("z", [128, 2, PIECE], F32)
        g2 = sb("g2", [128, 4], F32)
        st = sb("st", [128, CT, NB * NRC, 6], F32)
        mv = sb("mv", [128, CT, 2], F32)
        al = sb("al", [128, CT], F32)
        sm = sb("sm", [128, 12, CT], F32)
        py = [ctx.enter_context(nc.psum_tensor(f"py{k}", [128, 512], F32)) for k in range(4)]

        w_in = sem("w_in")
        w_signed = sem("w_signed")
        w_summed = sem("w_summed")
        pad_zero = sem("pad_zero")
        r_in = [[sem(f"r_in{slot}_{k}") for k in range(4)] for slot in range(3)]
        signed = sem("signed")
        y_filled = sem("y_filled")
        y_copied = sem("y_copied")
        stats_done = sem("stats_done")
        step = sem("step")
        root_in = sem("root_in")
        root_done = sem("root_done")
        coef_done = sem("coef_done")
        z_done = sem("z_done")
        r_done = sem("r_done")
        stored = sem("stored")
        block = ctx.enter_context(nc.Block())
        SM = (lambda k: sm[:, k, :])

        @block.sync
        def _(sp):
            for c in range(CT):
                sp.dma_start(xr[2][:, c, 0:TAPS * C], wt[c]).then_inc(w_in, 16)
            for c in range(CT):
                sp.dma_start(xr[1][:, c, 0:TAPS * C], wn[c]).then_inc(w_in, 16)
            sp.dma_start(g2[:], gb).then_inc(w_in, 16)

            x2v = x2d.rearrange("(t p n) -> t p n", p=128, n=CT * QC)

            def load(b, slot):
                per = CH // 4
                for k in range(4):
                    for c in range(CT):
                        sp.dma_start(xr[slot][:, c, k * PIECE:(k + 1) * PIECE].rearrange("p (j n) -> p j n", n=QC),
                                     x2v[1 + b * CH + k * per:1 + b * CH + (k + 1) * per, :, c * QC:(c + 1) * QC]
                                     .rearrange("j p n -> p j n")).then_inc(r_in[slot][k], 16)

            load(0, 0)
            sp.wait_ge(w_summed, CT)
            load(1, 1)
            sp.wait_ge(w_signed, CT)
            load(2, 2)
            sp.wait_ge(signed, CT * 2)
            load(3, 0)
            n = 0
            for b in LAST:
                for c in range(CT):
                    for k in range(4):
                        n += 1
                        sp.wait_ge(r_done, n)
                        slot = SLOT[b] if b else 1
                        sp.dma_start(out[b, c * 128:(c + 1) * 128, k * PIECE:(k + 1) * PIECE],
                                     xr[slot][:, c, k * PIECE:(k + 1) * PIECE]).then_inc(stored, 16)
                if b == LAST[0]:
                    sp.wait_ge(stored, 16 * n)
                    load(0, 1)
            sp.wait_ge(stored, 16 * n)

        @block.gpsimd
        def _(pool):
            nc.gpsimd.memset(pad[:].rearrange("p a c h w -> p (a c h w)"), 0.0).then_inc(pad_zero, 1)
            nc.gpsimd.memset(z[:], 0.0).then_inc(y_copied, 4)

        @block.scalar
        def _(act):
            act.wait_ge(w_in, 16 * (2 * CT + 1))
            for c in range(CT):
                nc.scalar.activation(ws[:, c, :, :].rearrange("p t o -> p (t o)"), xr[2][:, c, 0:TAPS * C],
                                     ACT.Sign).then_inc(w_signed, 1)
            act.wait_ge(pad_zero, 1)

            def signs(b, half):
                if b >= 1:
                    act.wait_ge(y_filled, ((b - 1) * 2 + half + 1) * (NRC // 2) * CT)
                for k in ((0, 1, 2), (1, 2, 3))[half]:
                    act.wait_ge(r_in[SLOT[b]][k], 32 if b < 3 else 64)
                for c in range(CT):
                    to = pad[:, half, c, 1:HH + 2, 1:1 + W] if half == 0 else pad[:, half, c, 0:HH + 1, 1:1 + W]
                    r0 = 0 if half == 0 else HH - 1
                    nc.scalar.activation(to, xr[SLOT[b]][:, c, r0 * W:(r0 + HH + 1) * W]
                                         .rearrange("p (h w) -> p h w", w=W), ACT.Sign).then_inc(signed, 1)

            signs(0, 0)
            for b in range(NB):
                for half in range(2):
                    if 2 * b + half + 1 < 2 * NB:
                        signs(b + half, 1 - half)
                    with act.Fori(0, NRC // 4) as h:
                        for u in range(2):
                            for o in range(CT):
                                n = (b * NRC + half * (NRC // 2) + u) * CT + o
                                act.wait_ge(y_filled, h * (2 * CT) + (n + 1))
                                nc.scalar.copy(Y[:, o, b, ds(h * (2 * RC * W) + (half * HH + u * RC) * W, RC * W)],
                                               py[u * CT + o][:]).then_inc(y_copied, 1)
            act.wait_ge(root_in, 1)
            nc.scalar.activation(SM(3), SM(2), ACT.Sqrt).then_inc(root_done, 1)
            act.wait_ge(coef_done, 2)
            n = 0
            for b in LAST:
                for c in range(CT):
                    for k in range(4):
                        if n >= 2:
                            act.wait_ge(r_done, n - 1)
                        nc.scalar.activation(z[:, n % 2, :], Y[:, c, b, k * PIECE:(k + 1) * PIECE], ACT.Identity,
                                             scale=sm[:, 7, c:c + 1], bias=sm[:, 9, c:c + 1]).then_inc(z_done, 1)
                        n += 1

        @block.tensor
        def _(pe):
            pe.wait_ge(w_signed, CT)
            for b in range(NB):
                for half in range(2):
                    pe.wait_ge(signed, CT * (2 * b + half + 1))
                    with pe.Fori(0, NRC // 4) as h:
                        for u in range(2):
                            for o in range(CT):
                                n = (b * NRC + half * (NRC // 2) + u) * CT + o
                                pe.wait_ge(y_copied, h * (2 * CT) + (n + 1))
                                for c in range(CT):
                                    for tap in range(TAPS):
                                        dy, dx = divmod(tap, 3)
                                        mm = pe.matmul(py[u * CT + o][:], ws[:, c, tap, o * 128:(o + 1) * 128],
                                                       pad[:, half, c, ds(h * (2 * RC) + (u * RC + dy), RC), dx:dx + W],
                                                       start=c == 0 and tap == 0,
                                                       stop=c == CT - 1 and tap == TAPS - 1)
                                mm.then_inc(y_filled, 1)

        @block.vector
        def _(dve):
            dve.wait_ge(w_in, 16 * (2 * CT + 1))
            for c in range(CT):
                nc.vector.tensor_reduce(al[:, c:c + 1], xr[1][:, c, 0:TAPS * C], AX.X, ALU.add,
                                        apply_absolute_value=True).then_inc(w_summed, 1)
            for b in range(NB):
                with dve.Fori(0, NRC // 2) as h:
                    for u in range(2):
                        for o in range(CT):
                            dve.wait_ge(y_copied, h * (2 * CT) + (b * NRC * CT + u * CT + o + 5))
                            nc.vector.bn_stats(st[:, o, ds(h * 2 + (b * NRC + u), 1), :].rearrange("p a s -> p (a s)"),
                                               Y[:, o, b, ds(h * (2 * RC * W) + u * RC * W, RC * W)]
                                               ).then_inc(stats_done, 1)
            dve.wait_ge(stats_done, NB * NRC * CT)
            dve.wait_ge(w_summed, CT)
            count = [0]

            def then(ins):
                count[0] += 1
                ins.then_inc(step, 1)
                dve.wait_ge(step, count[0])

            for c in range(CT):
                then(nc.vector.bn_aggr(mv[:, c, :], st[:, c, :, :].rearrange("p a s -> p (a s)")))
            then(nc.vector.tensor_scalar(SM(0), al[:], 1.0 / (C * TAPS), None, ALU.mult))
            then(nc.vector.tensor_tensor(SM(1), SM(0), mv[:, :, 1], ALU.mult))
            then(nc.vector.tensor_tensor(SM(10), SM(1), SM(0), ALU.mult))
            nc.vector.tensor_scalar(SM(2), SM(10), EPS, None, ALU.add).then_inc(root_in, 1)
            dve.wait_ge(root_done, 1)
            then(nc.vector.reciprocal(SM(4), SM(3)))
            then(nc.vector.tensor_tensor(SM(5), SM(4), SM(0), ALU.mult))
            then(nc.vector.tensor_tensor(SM(7), SM(5), g2[:, 0:2], ALU.mult))
            then(nc.vector.tensor_tensor(SM(8), SM(7), mv[:, :, 0], ALU.mult))
            nc.vector.tensor_tensor(SM(9), g2[:, 2:4], SM(8), ALU.subtract).then_inc(coef_done, 2)
            n = 0
            for b in LAST:
                for c in range(CT):
                    for k in range(4):
                        n += 1
                        dve.wait_ge(z_done, n)
                        slot = SLOT[b] if b else 1
                        dve.wait_ge(r_in[slot][k], 64 if b in (3, 0) else 32)
                        r = xr[slot][:, c, k * PIECE:(k + 1) * PIECE]
                        nc.vector.tensor_tensor(r, z[:, (n - 1) % 2, :], r, ALU.add).then_inc(r_done, 1)


def build(nc, x, w1r, cols, ident, wn, wt, gb, x2d, out):
    attention(nc, x, w1r, cols, ident, x2d)
    convolution(nc, wn, wt, gb, x2d, out)


def kernel(x, L0_conv_w1, L0_conv_b1, L1_conv_weights, L1_conv_gamma, L1_conv_beta):
    import concourse.bacc as bacc
    from concourse.bass_utils import run_bass_kernel_spmd as run

    f32 = np.float32
    w1, b1, w = (np.asarray(a) for a in (L0_conv_w1, L0_conv_b1, L1_conv_weights))
    w1r = np.zeros((C, 128), f32)
    cols = np.zeros((128, 8), f32)
    for r, (a, q) in enumerate(zip(SPLIT_A, SPLIT_B)):
        rows = slice(r * KF, (r + 1) * KF)
        w1r[:, rows] = w1.T
        cols[rows, 0] = b1
        for k, part in ((1, a), (3, q)):
            cols[rows, k] = -1.0 if part >= 2 else 0.0
            cols[rows, k + 1] = -1.0 if part >= 3 else 0.0
    cols[KE:KS, 0] = 1.0
    gb = np.concatenate([np.asarray(a).reshape(CT, 128).T for a in (L1_conv_gamma, L1_conv_beta)], axis=1)
    arrays = {
        "x": np.ascontiguousarray(np.asarray(x).reshape(-1)),
        "w1r": w1r, "cols": cols, "ident": np.eye(128, dtype=f32),
        "wn": np.ascontiguousarray(w.reshape(CT, 128, C * TAPS)),
        "wt": np.ascontiguousarray(w.reshape(C, CT, 128, TAPS).transpose(1, 2, 3, 0).reshape(CT, 128, TAPS * C)),
        "gb": np.ascontiguousarray(gb),
    }
    nc = bacc.Bacc("TRN2", target_bir_lowering=False, num_devices=1)
    args = [nc.dram_tensor(n, a.shape, F32, kind="ExternalInput").ap() for n, a in arrays.items()]
    args.append(nc.dram_tensor("x2", ((NB * CH + 1) * C * QC,), F32, kind="Internal").ap())
    args.append(nc.dram_tensor("out", (NB, C, N), F32, kind="ExternalOutput").ap())
    build(nc, *args)
    return run(nc, [arrays], core_ids=[0]).results[0]["out"].reshape(NB, C, H, W)
```

```python
from contextlib import ExitStack

import numpy as np
import concourse.bass as bass
from concourse import mybir

F32 = mybir.dt.float32
F32R = mybir.dt.float32r
BF16 = mybir.dt.bfloat16
I16 = mybir.dt.int16
ALU = mybir.AluOpType
ACT = mybir.ActivationFunctionType
AX = mybir.AxisListType
ds = bass.ds

NB, C, H, W = 4, 256, 64, 64
N = H * W
CT = C // 128
KF = 16
SPLIT_A = (1, 1, 2, 2, 1, 3)
SPLIT_B = (1, 2, 1, 2, 3, 1)
KE = KF * len(SPLIT_A)
KS = KE + 3
MT = N // 128
QC = 256
QT = QC // 128
CH = N // QC
GM = 4
G = MT // GM
RP = 4
SC = 512
SCN = QT * N // SC
SL = N // 512
XQ = 4
PROJECT_AT = (2, 4)
WC = 4
DEN = 10.0
EPS = 1e-5
TAPS = 9
PW = W + 2
UR = 16
UN = H // UR
UP = UR // 2
VK = 4
VLEN = VK * CT * UP * PW
PADLEN = CT * (UR + 2) * PW


def items_of(parts):
    out = []
    for g in range(G):
        if "scan" in parts:
            out += [(g, 0, "scan", 0), (g, 0, "scan", 1)]
        if g == 0:
            out += [(g, 4, "back", 0)]
        if g == 1 and "last" not in parts:
            out += [(g, 4, "shift", 0)]
        if "project" in parts and g in PROJECT_AT:
            out += [(g, 4, "project", PROJECT_AT.index(g))]
        if "spread" in parts and g < G - 1 or "border" in parts and g == G - 1:
            out += [(g, 4 if g == 0 else 3, "xt", 0), (g, 6 if g == 0 else 5, "xt", 1)]
    steps = [[] for _ in range(G)]
    for n, (g, *item) in enumerate(out):
        steps[g].append((*item, n % 2))
    return steps


def walk(eng, chunk):
    with eng.Fori(0, NB - 1) as b:
        chunk(b, 0, ("scan", "spread"))
        with eng.Fori(1, 3) as j:
            chunk(b, j, ("scan",))
        with eng.Fori(3, 3 + SL) as j:
            chunk(b, j, ("scan", "project"))
        with eng.Fori(3 + SL, CH - 2) as j:
            chunk(b, j, ("scan",))
        chunk(b, CH - 2, ("scan", "scan_next"))
        chunk(b, CH - 1, ("scan", "scan_next", "border"))
    chunk(NB - 1, 0, ("scan", "spread"))
    with eng.Fori(1, WC) as j:
        chunk(NB - 1, j, ("scan",))
    chunk(NB - 1, WC, ("scan", "weights"))
    with eng.Fori(WC + 1, CH - 2) as j:
        chunk(NB - 1, j, ("scan",))
    chunk(NB - 1, CH - 2, ("alpha",))
    chunk(NB - 1, CH - 1, ("last",))


def v_view(t):
    return t[:, 0:VLEN].rearrange("p (k c r w) -> p k c r w", k=VK, c=CT, w=PW)


def pad_view(t):
    return t[:, 0:PADLEN // 2].bitcast(BF16).rearrange("p (c r w) -> p c r w", c=CT, w=PW)


def load_x2(sp, x2d, b, to, sems):
    view = x2d.rearrange("(t p n) -> t p n", p=128, n=CT * QC)
    per = CH // UN
    for k in range(UN):
        for c in range(CT):
            t0 = 1 + b * CH + k * per
            sp.dma_start(to[:, c, k * UR * W:(k + 1) * UR * W].rearrange("p (j n) -> p j n", n=QC),
                         view[t0:t0 + per, :, c * QC:(c + 1) * QC].rearrange("j p n -> p j n")
                         ).then_inc(sems[k], 16)


def sign_unit(nc, act, b, u, r, r_in, due, pads, signed):
    lo, hi = max(u * UR - 1, 0), min((u + 1) * UR + 1, H)
    for k in range(lo // UR, (hi - 1) // UR + 1):
        act.wait_ge(r_in[k], due)
    row = lo - (u * UR - 1)
    for c in range(CT):
        nc.scalar.activation(pads[u % 2][:, c, row:row + hi - lo, 1:1 + W],
                             r[:, c, lo * W:hi * W].rearrange("p (h w) -> p h w", w=W),
                             ACT.Sign).then_inc(signed, 1)


def transform_unit(nc, pad, v, v_done):
    d = [pad[:, :, k:k + 2 * UP - 1:2, :] for k in range(4)]
    nc.gpsimd.tensor_tensor(v[:, 0], d[0], d[2], ALU.subtract)
    nc.gpsimd.tensor_tensor(v[:, 1], d[1], d[2], ALU.add)
    nc.gpsimd.tensor_tensor(v[:, 2], d[2], d[1], ALU.subtract)
    nc.gpsimd.tensor_tensor(v[:, 3], d[1], d[3], ALU.subtract).then_inc(v_done, 1)


def attention(nc, x, w1r, cols, ident, wn, wt, x2d, shared):
    xn, An, Bn, fw, tab, wk, al, sems = shared
    w_in, w_signed, wk_done, al_done, r0_in, pad_zero, signed, v_done = sems
    Fp, f1, f2 = fw[:, 0:512], fw[:, 512:768].bitcast(BF16), fw[:, 768:1024].bitcast(BF16)
    ta, tb = tab[:, 0:512], tab[:, 512:1024]
    pads = [pad_view(fw), pad_view(tab)]
    V = [v_view(An), v_view(Bn)]
    sw = [xn[:, c, TAPS * C:TAPS * C * 3 // 2].bitcast(BF16).rearrange("p (t o) -> p t o", o=C) for c in range(CT)]
    with ExitStack() as ctx:
        def sb(name, shape, dt):
            return ctx.enter_context(nc.sbuf_tensor(name, shape, dt))

        def ps(name, shape, dt=F32):
            return ctx.enter_context(nc.psum_tensor(name, shape, dt))

        def sem(name):
            return ctx.enter_context(nc.semaphore(name))

        xh = sb("xh", [128, MT, C + 2], F32R)
        xl = sb("xl", [128, MT, C], F32R)
        A = sb("A", [128, N], BF16)
        Bq = sb("Bq", [128, N], BF16)
        P = sb("P", [128, 2, GM * QC], F32)
        Ph = sb("Ph", [128, RP, GM, QC], F32R)
        Pl = sb("Pl", [128, RP, GM, QC], F32R)
        w1s = sb("w1s", [128, CT, 128], F32)
        col = sb("col", [128, 8], F32)
        idf = sb("idf", [128, 128], F32)
        idb = sb("idb", [128, 128], BF16)
        pm = sb("pm", [128, SCN], F32)
        negm = sb("negm", [128, QT], F32)
        ms = sb("ms", [128, 3 * QT], BF16)
        mr = sb("mr", [128, 2, QT], F32)
        mrow = sb("mrow", [3 * QT, 128], BF16)
        rd = sb("rd", [128, QT], F32)
        xs = sb("xs", [128, QT, C], F32)
        x2t = sb("x2t", [128, QT, C], F32)
        x2s = sb("x2s", [128, CT, QC], F32)

        pe2 = [ps(f"pe2_{k}", [128, GM * QC]) for k in range(2)]
        acc = [ps(f"acc_{i}", [128, 512]) for i in range(QT)]
        misc = [ps(f"misc_{k}", [128, 512]) for k in range(2)]

        outer_done = sem("outer_done")
        inner_done = sem("inner_done")
        const_in = sem("const_in")
        idb_done = sem("idb_done")
        fill_done = sem("fill_done")
        x_in = [sem(f"x_in{k}") for k in range(XQ)]
        f_filled = sem("f_filled")
        f_copied = sem("f_copied")
        split_step = sem("split_step")
        ab_done = sem("ab_done")
        border_done = sem("border_done")
        scan_filled = sem("scan_filled")
        scan_reduced = sem("scan_reduced")
        neg_done = sem("neg_done")
        ms_step = sem("ms_step")
        ms_done = sem("ms_done")
        m_filled = sem("m_filled")
        m_copied = sem("m_copied")
        m_stored = sem("m_stored")
        xt_filled = sem("xt_filled")
        xh_done = sem("xh_done")
        xl_done = sem("xl_done")
        e_done = sem("e_done")
        ph_done = sem("ph_done")
        pl_done = sem("pl_done")
        av_done = sem("av_done")
        acc_done = sem("acc_done")
        rd_done = sem("rd_done")
        evac_done = sem("evac_done")
        xs_done = sem("xs_done")
        back_filled = sem("back_filled")
        back_copied = sem("back_copied")
        x2_stored = sem("x2_stored")

        block = ctx.enter_context(nc.Block())

        @block.sync
        def _(sp):
            sp.dma_start(w1s[:], w1r.rearrange("(t p) k -> p t k", p=128)).then_inc(const_in, 16)
            sp.dma_start(col[:], cols).then_inc(const_in, 16)
            sp.dma_start(idf[:], ident).then_inc(const_in, 16)

            def load_x(at):
                batch = x[ds(at, C * N)].rearrange("(t p n) -> p t n", p=128, n=N)
                for k in range(XQ):
                    sp.dma_start(xn[:, :, k * (N // XQ):(k + 1) * (N // XQ)],
                                 batch[:, :, k * (N // XQ):(k + 1) * (N // XQ)]).then_inc(x_in[k], 16)

            def store_shift(due, dst):
                sp.wait_ge(m_copied, due)
                sp.dma_start(dst, mrow[:, :]).then_inc(m_stored, 16)

            def store_x2(due, at):
                sp.wait_ge(back_copied, due)
                sp.dma_start(x2d[ds(at, C * QC)].rearrange("(p n) -> p n", p=128),
                             x2s[:, :, :].rearrange("p c n -> p (c n)")).then_inc(x2_stored, 16)

            load_x(0)
            store_shift(1, Bn[KE:KS, 0:QC].rearrange("k (i c) -> k i c", i=QT))

            def ahead(value):
                return value if isinstance(value, int) else sp.snap(value)

            def chunk(b, j, parts):
                t = b * CH + j
                shift_due, back_due, x2_at = ahead(t + 2), ahead(t + 1), ahead(t * (C * QC))
                if "border" in parts:
                    dst = Bn[KE:KS, 0:QC]
                else:
                    dst = Bq[KE:KS, ds(ahead((j + 1) * QC), QC)] if "last" not in parts else None
                if "spread" in parts:
                    spread_due, x_at = ahead((b + 1) * (MT // 2)), ahead((b + 1) * (C * N))
                store_x2(back_due, x2_at)
                if "last" not in parts:
                    store_shift(shift_due, dst.rearrange("k (i c) -> k i c", i=QT))
                if "spread" in parts:
                    sp.wait_ge(xt_filled, spread_due)
                    if isinstance(b, int):
                        for c in range(CT):
                            sp.dma_start(xn[:, c, 0:TAPS * C], wt[c]).then_inc(w_in, 16)
                    else:
                        load_x(x_at)
                if "weights" in parts:
                    sp.wait_ge(w_signed, CT)
                    for c in range(CT):
                        sp.dma_start(xn[:, c, 0:TAPS * C], wn[c]).then_inc(w_in, 16)
                if "alpha" in parts:
                    sp.wait_ge(al_done, CT)
                    sp.wait_ge(wk_done, 1)
                    load_x2(sp, x2d, 0, xn, r0_in)

            walk(sp, chunk)
            store_x2(NB * CH + 1, NB * CH * C * QC)
            sp.wait_ge(x2_stored, 16 * (NB * CH + 1) + 1)

        @block.tensor
        def _(pe):
            pe.wait_ge(const_in, 48)
            pe.wait_ge(idb_done, 1)
            held = {0: None, 1: None}

            def take(bank):
                if held[bank]:
                    pe.wait_ge(*held[bank])

            def project(s, sl, half, bank):
                take(bank)
                for c in range(CT):
                    mm = pe.matmul(misc[bank][:, 0:256], w1s[:, c, :], xn[:, c, ds(sl * 512 + half * 256, 256)],
                                   start=c == 0, stop=c == CT - 1)
                mm.then_inc(f_filled, 1)
                held[bank] = (f_copied, s * 2 + (half + 1))

            def scan(T, i, q0, bank, a, bq):
                take(bank)
                mc = i // QT
                pe.matmul(misc[bank][:], a[0:KE, ds(q0 + (i % QT) * 128, 128)],
                          bq[0:KE, mc * SC:(mc + 1) * SC], start=True, stop=True).then_inc(scan_filled, 1)
                held[bank] = (scan_reduced, T * SCN + i + 1)

            def shift(T, bank):
                pe.wait_ge(ms_done, T + 1)
                take(bank)
                pe.transpose(misc[bank][0:3 * QT, 0:64].bitcast(BF16), ms[:, :], idb[:, :]).then_inc(m_filled, 1)
                held[bank] = (m_copied, T + 1)

            def back(t, bank):
                pe.wait_ge(evac_done, t * 2 + 2)
                take(bank)
                for c in range(CT):
                    for i in range(QT):
                        mm = pe.transpose(misc[bank][:, c * QC + i * 128:c * QC + (i + 1) * 128],
                                          x2t[:, i, c * 128:(c + 1) * 128], idf[:, :])
                mm.then_inc(back_filled, 1)
                held[bank] = (back_copied, t + 1)

            def spread(b, k, bank):
                take(bank)
                for h in range(2):
                    for c in range(CT):
                        m = 2 * k + h
                        mm = pe.transpose(misc[bank][:, h * C + c * 128:h * C + (c + 1) * 128],
                                          xn[:, c, m * 128:(m + 1) * 128], idf[:, :])
                mm.then_inc(xt_filled, 1)
                held[bank] = (xl_done, b * (MT // 2) + k + 1)

            def energy(g, c0):
                for k in range(GM):
                    m = g * GM + k
                    mm = pe.matmul(pe2[g % 2][:, k * QC:(k + 1) * QC], A[0:KS, m * 128:(m + 1) * 128],
                                   Bq[0:KS, ds(c0, QC)], start=True, stop=True)
                mm.then_inc(e_done, 1)

            def attend(t, g, between):
                for i in range(QT):
                    for k in range(GM):
                        between(i * GM + k)
                        if i == 0 and k == 0:
                            pe.wait_ge(pl_done, t * G + (g + 1))
                        if g == 0 and k == 0:
                            pe.wait_ge(evac_done, t * 2 + (i + 1))
                        m = g * GM + k
                        first, last = g == 0 and k == 0, g == G - 1 and k == GM - 1
                        ph = Ph[:, g % RP, k, i * 128:(i + 1) * 128]
                        pl = Pl[:, g % RP, k, i * 128:(i + 1) * 128]
                        pe.matmul(acc[i][:, 0:C + 2], ph, xh[:, m, :], start=first, stop=False)
                        pe.matmul(acc[i][:, 0:C], ph, xl[:, m, :], start=False, stop=False)
                        mm = pe.matmul(acc[i][:, 0:C + 2], pl, xh[:, m, :], start=False, stop=last)
                        if last and i < QT - 1:
                            mm.then_inc(acc_done, 1)
                        if k == GM - 1 and i == QT - 1:
                            mm.then_inc(av_done, 1)

            pe.wait_ge(fill_done, 1)
            for s in range(SL + 1):
                if s < SL:
                    if s % (SL // XQ) == 0:
                        pe.wait_ge(x_in[s // (SL // XQ)], 16)
                    for half in range(2):
                        project(s, s, half, half)
                if s > 0:
                    pe.wait_ge(ab_done, 4 * s + 1)
                    for i in range(QT):
                        scan(0, (s - 1) * QT + i, 0, i % 2, An, Bn)
            shift(0, 0)
            for i in range(SCN):
                scan(1, i, QC, (i + 1) % 2, An, Bn)
            spread(0, 0, 0)
            pe.wait_ge(border_done, 2)
            energy(0, 0)
            spread(0, 1, 1)
            energy(1, 0)

            def chunk(b, j, parts):
                t = b * CH + j
                items = items_of(parts)
                if "last" in parts:
                    held[0], held[1] = (back_copied, t), (m_copied, t + 1)
                elif "spread" in parts:
                    for k in range(2):
                        held[k] = (xl_done, b * (MT // 2) + (k + 1))
                else:
                    for k in range(2):
                        held[k] = (scan_reduced, (t + 1) * SCN + (SCN - 1 + k))
                for g in range(G):
                    if "last" not in parts or g < G - 2:
                        pe.wait_ge(ph_done, t * G + (g + 1))
                        if g < G - 2:
                            energy(g + 2, j * QC)
                        else:
                            if g == G - 2:
                                pe.wait_ge(m_stored, (t + 2) * 16)
                            if "border" in parts and g == G - 2:
                                pe.wait_ge(border_done, (b + 2) * 2)
                            energy(g + 2 - G, 0 if "border" in parts else (j + 1) * QC)

                    def between(slot):
                        for at, kind, k, bank in items[g]:
                            if at != slot:
                                continue
                            if kind == "xt" and "border" in parts:
                                for q in range(XQ):
                                    pe.wait_ge(x_in[q], (b + 2) * 16)
                                spread(b + 1, k, bank)
                            elif kind == "xt":
                                spread(b, 2 * (g + 1) + k, bank)
                            elif kind == "shift":
                                shift(t + 1, bank)
                            elif kind == "back":
                                back(t, bank)
                            elif kind == "project":
                                for q in range(XQ if k == 0 else 0):
                                    pe.wait_ge(x_in[q], (b + 2) * 16)
                                project((b + 1) * SL + (j - 3), j - 3, k, bank)
                            elif "scan_next" in parts:
                                scan(t + 2, 2 * g + k, (j - (CH - 2)) * QC, bank, An, Bn)
                            else:
                                scan(t + 2, 2 * g + k, (j + 2) * QC, bank, A, Bq)
                        if slot == 0 and "spread" in parts:
                            pe.wait_ge(xl_done, b * (MT // 2) + 2 * (g + 1))
                    attend(t, g, between)

            walk(pe, chunk)
            held[0], held[1] = (back_copied, NB * CH), None
            back(NB * CH, 0)

        @block.scalar
        def _(act):
            def exps(q, g):
                act.wait_ge(e_done, q + 1)
                if not (isinstance(q, int) and q < 2):
                    act.wait_ge(pl_done, q - 1)
                nc.scalar.activation(P[:, g % 2, :], pe2[g % 2][:], ACT.Exp)
                if not (isinstance(q, int) and q < 2):
                    act.wait_ge(av_done, q - 1)
                nc.scalar.activation(Ph[:, g % RP, :, :].rearrange("p k n -> p (k n)"), pe2[g % 2][:],
                                     ACT.Exp).then_inc(ph_done, 1)

            def project(s, half, bank):
                n = slice(half * 256, (half + 1) * 256)
                act.wait_ge(f_filled, s * 2 + (half + 1))
                if not (isinstance(s, int) and s == 0):
                    act.wait_ge(ab_done, s * 4 + (2 * half - 1))
                nc.scalar.activation(Fp[0:KS, n], misc[bank][0:KS, 0:256], ACT.Identity, bias=col[0:KS, 0:1])
                nc.scalar.activation(f1[0:KS, n], misc[bank][0:KS, 0:256], ACT.Identity,
                                     bias=col[0:KS, 0:1]).then_inc(f_copied, 1)

            def spread(b, k, bank, seen):
                act.wait_ge(xt_filled, b * (MT // 2) + k + 1)
                act.wait_ge(xs_done, seen + 1)
                nc.scalar.copy(xh[:, 2 * k:2 * k + 2, 0:C],
                               misc[bank][:].rearrange("p (m c) -> p m c", m=2)).then_inc(xh_done, 1)

            def back(t, bank):
                act.wait_ge(back_filled, t + 1)
                act.wait_ge(x2_stored, t * 16 + 1)
                nc.scalar.copy(x2s[:, :, :].rearrange("p c n -> p (c n)"), misc[bank][:]).then_inc(back_copied, 1)

            act.wait_ge(const_in, 48)
            for s in range(SL):
                for half in range(2):
                    project(s, half, half)
            for k in range(2):
                spread(0, k, k, 0)
                exps(k, k)

            def chunk(b, j, parts):
                t = b * CH + j
                items = items_of(parts)
                for g in range(G):
                    if "last" not in parts or g < G - 2:
                        exps(t * G + (g + 2), (g + 2) % G)
                    for _, kind, k, bank in items[g]:
                        if kind == "xt" and "border" in parts:
                            spread(b + 1, k, bank, b * CH + 2)
                        elif kind == "xt":
                            spread(b, 2 * (g + 1) + k, bank, b * CH)
                        elif kind == "back":
                            back(t, bank)
                        elif kind == "project":
                            project((b + 1) * SL + (j - 3), k, bank)
                    if "weights" in parts and g in (2, 4):
                        act.wait_ge(w_in, 16 * CT)
                        c = g // 4
                        nc.scalar.activation(sw[c].rearrange("p t o -> p (t o)"), xn[:, c, 0:TAPS * C],
                                             ACT.Sign).then_inc(w_signed, 1)
                    if "last" in parts and g >= G - 2:
                        act.wait_ge(pad_zero, 2)
                        sign_unit(nc, act, 0, g - (G - 2), xn, r0_in, 32, pads, signed)

            walk(act, chunk)
            back(NB * CH, 0)

        @block.vector
        def _(dve):
            dve.wait_ge(const_in, 48)
            nc.vector.memset(x2t[:], 0.0).then_inc(evac_done, 2)
            nc.vector.memset(f2[:], 0.0).then_inc(ab_done, 1)
            nc.vector.tensor_copy(idb[:], idf[:]).then_inc(idb_done, 1)

            def split_parts(s, half):
                n = slice(half * 256, (half + 1) * 256)
                dve.wait_ge(f_copied, s * 2 + (half + 1))
                dve.wait_ge(ab_done, s * 4 + (2 * half + 1))
                nc.vector.scalar_tensor_tensor(f2[0:KS, n], f1[0:KS, n], -1.0, Fp[0:KS, n],
                                               ALU.mult, ALU.add).then_inc(split_step, 1)
                nc.vector.scalar_tensor_tensor(ta[0:KS, n], f1[0:KS, n], col[0:KS, 1:2], Fp[0:KS, n],
                                               ALU.mult, ALU.add).then_inc(split_step, 1)
                nc.vector.scalar_tensor_tensor(tb[0:KS, n], f1[0:KS, n], col[0:KS, 3:4], Fp[0:KS, n],
                                               ALU.mult, ALU.add).then_inc(split_step, 1)

            def split_rows(s, sl, half):
                n = slice(half * 256, (half + 1) * 256)
                dve.wait_ge(split_step, s * 6 + (3 * half + 3))
                nc.vector.scalar_tensor_tensor(An[0:KS, ds(sl * 512 + half * 256, 256)], f2[0:KS, n],
                                               col[0:KS, 2:3], ta[0:KS, n], ALU.mult, ALU.add).then_inc(ab_done, 1)
                nc.vector.scalar_tensor_tensor(Bn[0:KS, ds(sl * 512 + half * 256, 256)], f2[0:KS, n],
                                               col[0:KS, 4:5], tb[0:KS, n], ALU.mult, ALU.add).then_inc(ab_done, 1)

            def scan(T, i, bank):
                dve.wait_ge(scan_filled, T * SCN + (i + 1))
                nc.vector.tensor_reduce(pm[:, i:i + 1], misc[bank][:], AX.X, ALU.max).then_inc(scan_reduced, 1)
                if i == SCN - 1:
                    dve.wait_ge(scan_reduced, T * SCN + SCN)
                    dve.wait_ge(ms_done, T)
                    nc.vector.tensor_reduce(negm[:], pm[:].rearrange("p (k i) -> p i k", i=QT), AX.X, ALU.max,
                                            negate=True).then_inc(neg_done, 1)

            def shift(T, bank):
                dve.wait_ge(m_filled, T + 1)
                dve.wait_ge(m_stored, T * 16)
                nc.vector.tensor_copy(mrow[:, :], misc[bank][0:3 * QT, 0:64].bitcast(BF16)).then_inc(m_copied, 1)

            def border(b, t):
                dve.wait_ge(ab_done, (b + 1) * (4 * SL) + 1)
                dve.wait_ge(m_stored, (t + 1) * 16)
                nc.vector.tensor_copy(A[0:KS, :], An[0:KS, 0:N]).then_inc(border_done, 1)
                nc.vector.tensor_copy(Bq[0:KS, :], Bn[0:KS, 0:N]).then_inc(border_done, 1)

            def spread(b, k, bank):
                dve.wait_ge(xh_done, b * (MT // 2) + k + 1)
                nc.vector.tensor_tensor(xl[:, 2 * k:2 * k + 2, :], misc[bank][:].rearrange("p (m c) -> p m c", m=2),
                                        xh[:, 2 * k:2 * k + 2, 0:C].bitcast(F32), ALU.subtract).then_inc(xl_done, 1)

            def lower(q, g):
                dve.wait_ge(ph_done, q + 1)
                nc.vector.tensor_tensor(Pl[:, g % RP, :, :].rearrange("p k n -> p (k n)"), P[:, g % 2, :],
                                        Ph[:, g % RP, :, :].rearrange("p k n -> p (k n)").bitcast(F32),
                                        ALU.subtract).then_inc(pl_done, 1)

            def evacuate(t, i):
                if i < QT - 1:
                    dve.wait_ge(acc_done, t + 1)
                else:
                    dve.wait_ge(av_done, t * G + (G + 2))
                nc.vector.reciprocal(rd[:, i:i + 1], acc[i][:, C:C + 1]).then_inc(rd_done, 1)
                dve.wait_ge(rd_done, t * 2 + (i + 1))
                dve.wait_ge(xs_done, t + 2)
                dve.wait_ge(back_filled, t + 1)
                nc.vector.scalar_tensor_tensor(x2t[:, i, :], acc[i][:, 0:C], rd[:, i:i + 1], xs[:, i, :],
                                               ALU.mult, ALU.add).then_inc(evac_done, 1)

            def make_weights():
                dve.wait_ge(w_signed, CT)
                for c in range(CT):
                    rows = [sw[c][:, 3 * k:3 * k + 3, :] for k in range(3)]
                    nc.vector.tensor_copy(wk[:, c, 0, :, :], rows[0])
                    nc.vector.tensor_copy(wk[:, c, 3, :, :], rows[2])
                    nc.vector.tensor_tensor(wk[:, c, 1, :, :], rows[0], rows[2], ALU.add).then_inc(outer_done, 1)
                    dve.wait_ge(outer_done, c + 1)
                    nc.vector.tensor_tensor(wk[:, c, 2, :, :], wk[:, c, 1, :, :], rows[1],
                                            ALU.subtract).then_inc(inner_done, 1)
                    dve.wait_ge(inner_done, c + 1)
                    last = nc.vector.tensor_tensor(wk[:, c, 1, :, :], wk[:, c, 1, :, :], rows[1], ALU.add)
                last.then_inc(wk_done, 1)

            for s in range(SL):
                for half in range(2):
                    split_parts(s, half)
                    split_rows(s, s, half)
                for i in range(QT):
                    scan(0, s * QT + i, i % 2)
            shift(0, 0)
            for i in range(SCN):
                scan(1, i, (i + 1) % 2)
            border(0, 0)
            for k in range(2):
                spread(0, k, k)
            lower(0, 0)

            def chunk(b, j, parts):
                t = b * CH + j
                items = items_of(parts)
                for g in range(G):
                    for _, kind, k, bank in items[g]:
                        if kind == "scan":
                            scan(t + 2, 2 * g + k, bank)
                    if "last" not in parts or g < G - 1:
                        lower(t * G + (g + 1), (g + 1) % G)
                    for _, kind, k, bank in items[g]:
                        if kind == "xt" and "border" in parts:
                            spread(b + 1, k, bank)
                        elif kind == "xt":
                            spread(b, 2 * (g + 1) + k, bank)
                        elif kind == "shift":
                            shift(t + 1, bank)
                    if "project" in parts and g - 1 in PROJECT_AT:
                        split_parts((b + 1) * SL + (j - 3), PROJECT_AT.index(g - 1))
                    if "project" in parts and g - 2 in PROJECT_AT:
                        split_rows((b + 1) * SL + (j - 3), j - 3, PROJECT_AT.index(g - 2))
                    if "border" in parts and g == G - 3:
                        dve.wait_ge(e_done, (t + 1) * G)
                        border(b + 1, t + 1)
                    if g == G - 1:
                        for i in range(QT):
                            evacuate(t, i)
                    if "weights" in parts and g == G - 1:
                        make_weights()
                    if "alpha" in parts and g in (1, 3):
                        dve.wait_ge(w_in, 16 * 2 * CT)
                        c = g // 3
                        nc.vector.tensor_reduce(al[:, c:c + 1], xn[:, c, 0:TAPS * C], AX.X, ALU.add,
                                                apply_absolute_value=True).then_inc(al_done, 1)

            walk(dve, chunk)

        @block.gpsimd
        def _(pool):
            nc.gpsimd.memset(xh[:, :, C:C + 2].bitcast(F32), DEN).then_inc(fill_done, 1)
            pool.wait_ge(fill_done, 1)
            nc.gpsimd.memset(mr[:], 0.0).then_inc(av_done, 2)
            nc.gpsimd.memset(xs[:], 0.0).then_inc(xs_done, 1)
            nc.gpsimd.memset(x2s[:], 0.0).then_inc(x2_stored, 1)

            pool.wait_ge(av_done, 2)

            def parts_of_max(T):
                pool.wait_ge(neg_done, T + 1)
                pool.wait_ge(m_filled, T)
                nc.gpsimd.tensor_tensor(ms[:, 0:QT], negm[:], mr[:, 1, :], ALU.add).then_inc(ms_step, 1)
                pool.wait_ge(ms_step, T * 3 + 1)
                nc.gpsimd.tensor_tensor(mr[:, 0, :], negm[:], ms[:, 0:QT], ALU.subtract).then_inc(ms_step, 1)
                pool.wait_ge(ms_step, T * 3 + 2)
                nc.gpsimd.tensor_tensor(ms[:, QT:2 * QT], mr[:, 0, :], mr[:, 1, :], ALU.add).then_inc(ms_step, 1)
                pool.wait_ge(ms_step, T * 3 + 3)
                nc.gpsimd.tensor_tensor(ms[:, 2 * QT:3 * QT], mr[:, 0, :], ms[:, QT:2 * QT],
                                        ALU.subtract).then_inc(ms_done, 1)

            parts_of_max(0)

            def chunk(b, j, parts):
                t = b * CH + j
                if "last" not in parts:
                    parts_of_max(t + 1)
                pool.wait_ge(evac_done, t * 2 + 2)
                if "spread" in parts:
                    pool.wait_ge(xl_done, b * (MT // 2) + 2)
                else:
                    pool.wait_ge(xl_done, (b + 1) * (MT // 2))
                nc.gpsimd.tensor_tensor(xs[:], xh[:, ds(j * QT, QT), 0:C].bitcast(F32),
                                        xl[:, ds(j * QT, QT), :].bitcast(F32), ALU.add).then_inc(xs_done, 1)
                if "last" in parts:
                    for k in range(2):
                        nc.gpsimd.memset((fw, tab)[k][:], 0.0).then_inc(pad_zero, 1)
                    for u in range(2):
                        pool.wait_ge(signed, CT * (u + 1))
                        transform_unit(nc, pads[u], V[u], v_done)

            walk(pool, chunk)


def convolution(nc, gb, x2d, out, shared):
    SLOT = (0, 1, 2, 0)
    LAST = (1, 2, 3, 0)
    PIECE = UR * W
    xn, An, Bn, fw, tab, wk, al, sems = shared
    w_in, w_signed, wk_done, al_done, r0_in, pad_zero, signed, v_done = sems
    pads = [pad_view(fw), pad_view(tab)]
    V = [v_view(An), v_view(Bn)]
    z = [t[:, 0:2 * PIECE].bitcast(F32) for t in (An, Bn)]
    with ExitStack() as ctx:
        def sb(name, shape, dt):
            return ctx.enter_context(nc.sbuf_tensor(name, shape, dt))

        def sem(name):
            return ctx.enter_context(nc.semaphore(name))

        xr = [xn, sb("xr1", [128, CT, N], F32), sb("xr2", [128, CT, N], F32)]
        Y = sb("Y", [128, CT, NB * N], I16)
        m1 = sb("m1", [128, CT, UP * W], I16)
        plus = sb("plus", [128, UP * W], I16)
        minus = sb("minus", [128, UP * W], I16)
        none = sb("none", [128, CT, 1, PW], BF16)
        g2 = sb("g2", [128, 4], F32)
        st = sb("st", [128, CT, NB * UN * 2, 6], F32)
        mv = sb("mv", [128, CT, 2], F32)
        sm = sb("sm", [128, 12, CT], F32)
        pm = [[ctx.enter_context(nc.psum_tensor(f"pm{o}_{k}", [128, UP * W], F32)) for k in range(VK)]
              for o in range(CT)]

        g_in = sem("g_in")
        r_in = [r0_in] + [[sem(f"r_in{slot}_{k}") for k in range(UN)] for slot in (1, 2)]
        m_filled = sem("conv_filled")
        m1_done = sem("m1_done")
        half_done = sem("half_done")
        y_done = sem("y_done")
        edge_done = sem("edge_done")
        none_done = sem("none_done")
        stats_done = sem("stats_done")
        step = sem("step")
        root_in = sem("root_in")
        root_done = sem("root_done")
        coef_done = sem("coef_done")
        z_done = sem("z_done")
        r_done = sem("r_done")
        stored = sem("stored")
        block = ctx.enter_context(nc.Block())
        SM = (lambda k: sm[:, k, :])
        ORDER = (1, 2, 0, 3)

        @block.sync
        def _(sp):
            sp.dma_start(g2[:], gb).then_inc(g_in, 16)
            load_x2(sp, x2d, 1, xr[1], r_in[1])
            load_x2(sp, x2d, 2, xr[2], r_in[2])
            sp.wait_ge(signed, CT * UN)
            load_x2(sp, x2d, 3, xr[0], r_in[0])
            n = 0
            for b in LAST:
                slot = SLOT[b] if b else 1
                for c in range(CT):
                    for k in range(UN):
                        n += 1
                        sp.wait_ge(r_done, n)
                        sp.dma_start(out[b, c * 128:(c + 1) * 128, k * PIECE:(k + 1) * PIECE],
                                     xr[slot][:, c, k * PIECE:(k + 1) * PIECE]).then_inc(stored, 16)
                if b == LAST[0]:
                    sp.wait_ge(stored, 16 * n)
                    load_x2(sp, x2d, 0, xr[1], r_in[1])
            sp.wait_ge(stored, 16 * n)

        @block.gpsimd
        def _(pool):
            nc.gpsimd.memset(plus[:], 0.0).then_inc(y_done, 2)
            nc.gpsimd.memset(none[:], 0.0).then_inc(none_done, 1)
            pool.wait_ge(none_done, 1)

            def unit(U, u, edges):
                pool.wait_ge(m_filled, (U - 1) * (VK * CT))
                if u == 0:
                    nc.gpsimd.tensor_tensor(pads[0][:, :, 0:1, :], none[:], none[:], ALU.add).then_inc(edge_done, 1)
                    pool.wait_ge(edge_done, edges)
                if u == UN - 1:
                    nc.gpsimd.tensor_tensor(pads[1][:, :, UR + 1:UR + 2, :], none[:], none[:],
                                            ALU.add).then_inc(edge_done, 1)
                    pool.wait_ge(edge_done, edges)
                pool.wait_ge(signed, U * CT + CT)
                transform_unit(nc, pads[u % 2], V[u % 2], v_done)

            unit(2, 2, 0)
            unit(3, 3, 1)
            with pool.Fori(1, NB) as b:
                for u in range(UN):
                    unit(b * UN + u, u, b * 2 + (0 if u == 0 else 1))

        @block.scalar
        def _(act):
            for U in range(NB * UN):
                if U + 2 < NB * UN:
                    b, u = divmod(U + 2, UN)
                    act.wait_ge(v_done, U + 1)
                    sign_unit(nc, act, b, u, xr[SLOT[b]], r_in[SLOT[b]], 64 if b == 3 else 32, pads, signed)
                for o in range(CT):
                    n = U * CT + o
                    act.wait_ge(m_filled, VK * n + 1)
                    nc.scalar.copy(m1[:, o, :], pm[o][1][:]).then_inc(m1_done, 1)
            act.wait_ge(root_in, 1)
            nc.scalar.activation(SM(3), SM(2), ACT.Sqrt).then_inc(root_done, 1)
            act.wait_ge(coef_done, 2)
            act.wait_ge(m_filled, NB * UN * CT * VK)
            n = 0
            for b in LAST:
                for c in range(CT):
                    for k in range(UN):
                        if n >= 2:
                            act.wait_ge(r_done, n - 1)
                        nc.scalar.activation(z[n % 2], Y[:, c, b * N + k * PIECE:b * N + (k + 1) * PIECE],
                                             ACT.Identity, scale=sm[:, 7, c:c + 1],
                                             bias=sm[:, 9, c:c + 1]).then_inc(z_done, 1)
                        n += 1

        @block.tensor
        def _(pe):
            pe.wait_ge(wk_done, 1)
            with pe.Fori(0, NB * UN // 2) as h:
                for u in range(2):
                    pe.wait_ge(v_done, h * 2 + (u + 1))
                    for o in range(CT):
                        pe.wait_ge(y_done, h * (2 * CT) + (u * CT + o + 1))
                        for k in ORDER:
                            for c in range(CT):
                                for dx in range(3):
                                    mm = pe.matmul(pm[o][k][:], wk[:, c, k, dx, o * 128:(o + 1) * 128],
                                                   V[u][:, k, c, :, dx:dx + W],
                                                   start=c == 0 and dx == 0, stop=c == CT - 1 and dx == 2)
                            mm.then_inc(m_filled, 1)

        @block.vector
        def _(dve):
            with dve.Fori(0, NB * UN // 2) as h:
                for u in range(2):
                    for o in range(CT):
                        n = u * CT + o
                        y = Y[:, o, ds(h * (2 * PIECE) + u * PIECE, PIECE)]
                        rows = y.rearrange("p (r two w) -> p r two w", two=2, w=W)
                        dve.wait_ge(m1_done, h * (2 * CT) + (n + 1))
                        dve.wait_ge(m_filled, h * (2 * CT * VK) + (n * VK + 2))
                        nc.vector.tensor_tensor(plus[:], pm[o][2][:], m1[:, o, :], ALU.add).then_inc(half_done, 1)
                        nc.vector.tensor_tensor(minus[:], m1[:, o, :], pm[o][2][:],
                                                ALU.subtract).then_inc(half_done, 1)
                        dve.wait_ge(half_done, h * (4 * CT) + (2 * n + 2))
                        dve.wait_ge(m_filled, h * (2 * CT * VK) + (n * VK + 3))
                        nc.vector.scalar_tensor_tensor(
                            rows[:, :, 0, :], plus[:].rearrange("p (r w) -> p r w", w=W), 0.5,
                            pm[o][0][:].rearrange("p (r w) -> p r w", w=W), ALU.mult, ALU.add)
                        dve.wait_ge(m_filled, h * (2 * CT * VK) + (n * VK + 4))
                        nc.vector.scalar_tensor_tensor(
                            rows[:, :, 1, :], minus[:].rearrange("p (r w) -> p r w", w=W), 0.5,
                            pm[o][3][:].rearrange("p (r w) -> p r w", w=W), ALU.mult, ALU.subtract
                        ).then_inc(y_done, 1)
                        dve.wait_ge(y_done, h * (2 * CT) + (n + 3))
                        for k in range(2):
                            nc.vector.bn_stats(st[:, o, ds(h * 4 + (u * 2 + k), 1), :].rearrange("p a s -> p (a s)"),
                                               Y[:, o, ds(h * (2 * PIECE) + (u * PIECE + k * 512), 512)]
                                               ).then_inc(stats_done, 1)
            dve.wait_ge(stats_done, NB * UN * CT * 2)
            dve.wait_ge(al_done, CT)
            dve.wait_ge(g_in, 16)
            count = [0]

            def then(ins):
                count[0] += 1
                ins.then_inc(step, 1)
                dve.wait_ge(step, count[0])

            for c in range(CT):
                then(nc.vector.bn_aggr(mv[:, c, :], st[:, c, :, :].rearrange("p a s -> p (a s)")))
            then(nc.vector.tensor_scalar(SM(0), al[:], 1.0 / (C * TAPS), None, ALU.mult))
            then(nc.vector.tensor_tensor(SM(1), SM(0), mv[:, :, 1], ALU.mult))
            then(nc.vector.tensor_tensor(SM(10), SM(1), SM(0), ALU.mult))
            nc.vector.tensor_scalar(SM(2), SM(10), EPS, None, ALU.add).then_inc(root_in, 1)
            dve.wait_ge(root_done, 1)
            then(nc.vector.reciprocal(SM(4), SM(3)))
            then(nc.vector.tensor_tensor(SM(5), SM(4), SM(0), ALU.mult))
            then(nc.vector.tensor_tensor(SM(7), SM(5), g2[:, 0:2], ALU.mult))
            then(nc.vector.tensor_tensor(SM(8), SM(7), mv[:, :, 0], ALU.mult))
            nc.vector.tensor_tensor(SM(9), g2[:, 2:4], SM(8), ALU.subtract).then_inc(coef_done, 2)
            n = 0
            for b in LAST:
                slot = SLOT[b] if b else 1
                for c in range(CT):
                    for k in range(UN):
                        n += 1
                        dve.wait_ge(z_done, n)
                        dve.wait_ge(r_in[slot][k], 64 if b in (3, 0) else 32)
                        r = xr[slot][:, c, k * PIECE:(k + 1) * PIECE]
                        nc.vector.tensor_tensor(r, z[(n - 1) % 2], r, ALU.add).then_inc(r_done, 1)


def build(nc, x, w1r, cols, ident, wn, wt, gb, x2d, out):
    with ExitStack() as ctx:
        def sb(name, shape, dt):
            return ctx.enter_context(nc.sbuf_tensor(name, shape, dt))

        def sem(name):
            return ctx.enter_context(nc.semaphore(name))

        xn = sb("xn", [128, CT, N], F32)
        An = sb("An", [128, VLEN], BF16)
        Bn = sb("Bn", [128, VLEN], BF16)
        fw = sb("fw", [128, PADLEN // 2], F32)
        tab = sb("tab", [128, PADLEN // 2], F32)
        wk = sb("wk", [128, CT, VK, 3, C], BF16)
        al = sb("al", [128, CT], F32)
        sems = (sem("w_in"), sem("w_signed"), sem("wk_done"), sem("al_done"),
                [sem(f"r_in0_{k}") for k in range(UN)], sem("pad_zero"), sem("signed"), sem("v_done"))
        shared = (xn, An, Bn, fw, tab, wk, al, sems)
        attention(nc, x, w1r, cols, ident, wn, wt, x2d, shared)
        convolution(nc, gb, x2d, out, shared)


def kernel(x, L0_conv_w1, L0_conv_b1, L1_conv_weights, L1_conv_gamma, L1_conv_beta):
    import concourse.bacc as bacc
    from concourse.bass_utils import run_bass_kernel_spmd as run

    f32 = np.float32
    w1, b1, w = (np.asarray(a) for a in (L0_conv_w1, L0_conv_b1, L1_conv_weights))
    w1r = np.zeros((C, 128), f32)
    cols = np.zeros((128, 8), f32)
    for r, (a, q) in enumerate(zip(SPLIT_A, SPLIT_B)):
        rows = slice(r * KF, (r + 1) * KF)
        w1r[:, rows] = w1.T
        cols[rows, 0] = b1
        for k, part in ((1, a), (3, q)):
            cols[rows, k] = -1.0 if part >= 2 else 0.0
            cols[rows, k + 1] = -1.0 if part >= 3 else 0.0
    cols[KE:KS, 0] = 1.0
    gb = np.concatenate([np.asarray(a).reshape(CT, 128).T for a in (L1_conv_gamma, L1_conv_beta)], axis=1)
    arrays = {
        "x": np.ascontiguousarray(np.asarray(x).reshape(-1)),
        "w1r": w1r, "cols": cols, "ident": np.eye(128, dtype=f32),
        "wn": np.ascontiguousarray(w.reshape(CT, 128, C * TAPS)),
        "wt": np.ascontiguousarray(w.reshape(C, CT, 128, TAPS).transpose(1, 2, 3, 0).reshape(CT, 128, TAPS * C)),
        "gb": np.ascontiguousarray(gb),
    }
    nc = bacc.Bacc("TRN2", target_bir_lowering=False, num_devices=1)
    args = [nc.dram_tensor(n, a.shape, F32, kind="ExternalInput").ap() for n, a in arrays.items()]
    args.append(nc.dram_tensor("x2", ((NB * CH + 1) * C * QC,), F32, kind="Internal").ap())
    args.append(nc.dram_tensor("out", (NB, C, N), F32, kind="ExternalOutput").ap())
    build(nc, *args)
    return run(nc, [arrays], core_ids=[0]).results[0]["out"].reshape(NB, C, H, W)
```

```python
from contextlib import ExitStack

import numpy as np
import concourse.bass as bass
from concourse import mybir

F32 = mybir.dt.float32
F32R = mybir.dt.float32r
BF16 = mybir.dt.bfloat16
I16 = mybir.dt.int16
ALU = mybir.AluOpType
ACT = mybir.ActivationFunctionType
AX = mybir.AxisListType
ds = bass.ds

NB, C, H, W = 4, 256, 64, 64
N = H * W
CT = C // 128
KF = 16
SPLIT_A = (1, 1, 2, 2, 1, 3)
SPLIT_B = (1, 2, 1, 2, 3, 1)
KE = KF * len(SPLIT_A)
KS = KE + 3
MT = N // 128
QC = 256
QT = QC // 128
CH = N // QC
GM = 4
G = MT // GM
RP = 4
SC = 512
SCN = QT * N // SC
SL = N // 512
XB = 3
XQ = SL
PROJECT_AT = (2, 4)
WC = 4
DEN = 10.0
EPS = 1e-5
TAPS = 9
PW = W + 2
UR = 16
UN = H // UR
UP = UR // 2
VK = 4
VLEN = VK * CT * UP * PW
PADLEN = CT * (UR + 2) * PW



def items_of(parts):
    out = []
    for g in range(G):
        if "scan" in parts:
            out += [(g, 0, "scan", 0), (g, 0, "scan", 1)]
        if g == 0:
            out += [(g, 4, "back", 0)]
        if g == 1 and "last" not in parts:
            out += [(g, 4, "shift", 0)]
        if "project" in parts and g in PROJECT_AT:
            out += [(g, 4, "project", PROJECT_AT.index(g))]
    steps = [[] for _ in range(G)]
    for n, (g, *item) in enumerate(out):
        steps[g].append((*item, n % 2))
    return steps


def walk(eng, chunk):
    with eng.Fori(0, NB - 1) as b:
        chunk(b, 0, ("scan", "fresh"))
        with eng.Fori(1, 3) as j:
            chunk(b, j, ("scan",))
        with eng.Fori(3, 3 + SL) as j:
            chunk(b, j, ("scan", "project"))
        with eng.Fori(3 + SL, CH - 2) as j:
            chunk(b, j, ("scan",))
        chunk(b, CH - 2, ("scan", "scan_next"))
        chunk(b, CH - 1, ("scan", "scan_next", "border"))
    chunk(NB - 1, 0, ("scan", "fresh"))
    with eng.Fori(1, WC) as j:
        chunk(NB - 1, j, ("scan",))
    chunk(NB - 1, WC, ("scan", "weights"))
    with eng.Fori(WC + 1, CH - 2) as j:
        chunk(NB - 1, j, ("scan",))
    chunk(NB - 1, CH - 2, ("alpha",))
    chunk(NB - 1, CH - 1, ("last",))


def v_view(t):
    return t[:, 0:VLEN].rearrange("p (k c r w) -> p k c r w", k=VK, c=CT, w=PW)


def pad_view(t):
    return t[:, 0:PADLEN // 2].bitcast(BF16).rearrange("p (c r w) -> p c r w", c=CT, w=PW)


def load_x2(sp, x2d, b, to, sems):
    view = x2d.rearrange("(t p n) -> t p n", p=128, n=CT * QC)
    per = CH // UN
    for k in range(UN):
        for c in range(CT):
            t0 = 1 + b * CH + k * per
            sp.dma_start(to[:, c, k * UR * W:(k + 1) * UR * W].rearrange("p (j n) -> p j n", n=QC),
                         view[t0:t0 + per, :, c * QC:(c + 1) * QC].rearrange("j p n -> p j n")
                         ).then_inc(sems[k], 16)


def sign_unit(nc, act, b, u, r, r_in, due, pads, signed, tiles=range(CT)):
    lo, hi = max(u * UR - 1, 0), min((u + 1) * UR + 1, H)
    for k in range(lo // UR, (hi - 1) // UR + 1):
        act.wait_ge(r_in[k], due)
    row = lo - (u * UR - 1)
    for c in tiles:
        nc.scalar.activation(pads[u % 2][:, c, row:row + hi - lo, 1:1 + W],
                             r[:, c, lo * W:hi * W].rearrange("p (h w) -> p h w", w=W),
                             ACT.Sign).then_inc(signed, 1)


def transform_unit(nc, pad, v, v_done):
    d = [pad[:, :, k:k + 2 * UP - 1:2, :] for k in range(4)]
    nc.gpsimd.tensor_tensor(v[:, 0], d[0], d[2], ALU.subtract)
    nc.gpsimd.tensor_tensor(v[:, 1], d[1], d[2], ALU.add)
    nc.gpsimd.tensor_tensor(v[:, 2], d[2], d[1], ALU.subtract)
    nc.gpsimd.tensor_tensor(v[:, 3], d[1], d[3], ALU.subtract).then_inc(v_done, 1)


def attention(nc, x, xt, w1r, cols, ident, wn, wt, x2d, shared):
    xn, An, Bn, fw, tab, wk, x2s, al, sems = shared
    w_in, w_signed, wk_done, al_done, r0_in, pad_zero, signed, v_done, x2_stored = sems
    Fp, f1, f2 = fw[:, 0:512], fw[:, 512:768].bitcast(BF16), fw[:, 768:1024].bitcast(BF16)
    ta, tb = tab[:, 0:512], tab[:, 512:1024]
    pads = [pad_view(fw), pad_view(tab)]
    V = [v_view(An), v_view(Bn)]
    sw = [xn[:, c, TAPS * C:TAPS * C * 3 // 2].bitcast(BF16).rearrange("p (t o) -> p t o", o=C) for c in range(CT)]
    with ExitStack() as ctx:
        def sb(name, shape, dt):
            return ctx.enter_context(nc.sbuf_tensor(name, shape, dt))

        def ps(name, shape, dt=F32):
            return ctx.enter_context(nc.psum_tensor(name, shape, dt))

        def sem(name):
            return ctx.enter_context(nc.semaphore(name))

        xh = sb("xh", [128, MT, C + 2], F32R)
        xl = sb("xl", [128, MT, C], F32R)
        landed = [wk[:, :, :, :, :].rearrange("p c k x o -> p (c k x o)")[
            :, m * 2 * GM * C:(m + 1) * 2 * GM * C].bitcast(F32) for m in range(XB)]
        A = sb("A", [128, N], BF16)
        Bq = sb("Bq", [128, N], BF16)
        P = sb("P", [128, 2, GM * QC], F32)
        Ph = sb("Ph", [128, RP, GM, QC], F32R)
        Pl = sb("Pl", [128, RP, GM, QC], F32R)
        w1s = sb("w1s", [128, CT, 128], F32)
        col = sb("col", [128, 8], F32)
        idf = sb("idf", [128, 128], F32)
        idb = sb("idb", [128, 128], BF16)
        pm = sb("pm", [128, SCN], F32)
        negm = sb("negm", [128, QT], F32)
        ms = sb("ms", [128, 3 * QT], BF16)
        mr = sb("mr", [128, 2, QT], F32)
        mrow = sb("mrow", [3 * QT, 128], BF16)
        rd = sb("rd", [128, QT], F32)
        warm = sb("warm", [128, 1], F32)
        xs = sb("xs", [128, QT, C], F32)
        x2t = sb("x2t", [128, QT, C], F32)

        pe2 = [ps(f"pe2_{k}", [128, GM * QC]) for k in range(2)]
        acc = [ps(f"acc_{i}", [128, 512]) for i in range(QT)]
        misc = [ps(f"misc_{k}", [128, 512]) for k in range(2)]
        banks = misc + acc + [pe2[1]]
        SHIFT0 = 4

        outer_done = sem("outer_done")
        inner_done = sem("inner_done")
        w1_in = sem("w1_in")
        const_in = sem("const_in")
        idb_done = sem("idb_done")
        fill_done = sem("fill_done")
        x_in = [sem(f"x_in{k}") for k in range(XQ)]
        f_filled = sem("f_filled")
        f_copied = sem("f_copied")
        split_step = sem("split_step")
        first_f2 = sem("first_f2")
        warm_done = sem("warm_done")
        ab_done = sem("ab_done")
        border_done = sem("border_done")
        scan_filled = sem("scan_filled")
        scan_reduced = sem("scan_reduced")
        neg_done = sem("neg_done")
        ms_step = sem("ms_step")
        ms_done = sem("ms_done")
        m_filled = sem("m_filled")
        m_copied = sem("m_copied")
        m_stored = sem("m_stored")
        xt_in = [sem(f"xt_in{m}") for m in range(XB)]
        xh_done = sem("xh_done")
        xl_done = sem("xl_done")
        e_done = sem("e_done")
        ph_done = sem("ph_done")
        pl_done = sem("pl_done")
        av_done = sem("av_done")
        acc_done = sem("acc_done")
        rd_done = sem("rd_done")
        evac_done = sem("evac_done")
        xs_done = sem("xs_done")
        back_filled = sem("back_filled")
        back_copied = sem("back_copied")

        block = ctx.enter_context(nc.Block())

        @block.sync
        def _(sp):
            def load_x(at, pieces=range(XQ)):
                batch = x[ds(at, C * N)].rearrange("(t p n) -> p t n", p=128, n=N)
                for k in pieces:
                    sp.dma_start(xn[:, :, k * (N // XQ):(k + 1) * (N // XQ)],
                                 batch[:, :, k * (N // XQ):(k + 1) * (N // XQ)]).then_inc(x_in[k], 16)

            sp.dma_start(w1s[:], w1r.rearrange("(t p) k -> p t k", p=128)).then_inc(w1_in, 16)
            load_x(0, range(1))
            sp.dma_start(col[:], cols).then_inc(const_in, 16)
            sp.dma_start(idf[:], ident).then_inc(const_in, 16)
            load_x(0, range(1, XQ))

            def load_xt(g, at, due):
                if due is not None:
                    sp.wait_ge(xl_done, due)
                sp.dma_start(landed[g % XB], xt[ds(at, GM * 128 * C)].rearrange("(p n) -> p n", p=128)
                             ).then_inc(xt_in[g % XB], 16)

            def store_shift(due, dst):
                sp.wait_ge(m_copied, due)
                sp.dma_start(dst, mrow[:, :]).then_inc(m_stored, 16)

            def store_x2(due, at):
                sp.wait_ge(back_copied, due)
                sp.dma_start(x2d[ds(at, C * QC)].rearrange("(p n) -> p n", p=128),
                             x2s[:, :, :].rearrange("p c n -> p (c n)")).then_inc(x2_stored, 16)

            for g in range(G):
                load_xt(g, g * (GM * 128 * C), g - XB + 1 if g >= XB else None)
            sp.wait_ge(border_done, 2)
            store_shift(1, Bq[KE:KS, 0:QC].rearrange("k (i c) -> k i c", i=QT))

            def ahead(value):
                return value if isinstance(value, int) else sp.snap(value)

            def chunk(b, j, parts):
                t = b * CH + j
                shift_due, back_due, x2_at = ahead(t + 2), ahead(t + 1), ahead(t * (C * QC))
                if "border" in parts:
                    dst = Bn[KE:KS, 0:QC]
                else:
                    dst = Bq[KE:KS, ds(ahead((j + 1) * QC), QC)] if "last" not in parts else None
                if "fresh" in parts:
                    projected_due, x_at = ahead((b + 1) * (2 * SL)), ahead((b + 1) * (C * N))
                if "border" in parts:
                    xt_due = [ahead((b + 1) * G + max(g - XB + 1, 0)) for g in range(G)]
                    xt_at = [ahead((b + 1) * (C * N) + g * (GM * 128 * C)) for g in range(G)]
                store_x2(back_due, x2_at)
                if "last" not in parts:
                    store_shift(shift_due, dst.rearrange("k (i c) -> k i c", i=QT))
                if "fresh" in parts:
                    sp.wait_ge(f_filled, projected_due)
                    if isinstance(b, int):
                        for c in range(CT):
                            sp.dma_start(xn[:, c, 0:TAPS * C], wt[c]).then_inc(w_in, 16)
                    else:
                        load_x(x_at)
                if "border" in parts:
                    for g in range(G):
                        load_xt(g, xt_at[g], xt_due[g])
                if "weights" in parts:
                    sp.wait_ge(w_signed, CT)
                    for c in range(CT):
                        sp.dma_start(xn[:, c, 0:TAPS * C], wn[c]).then_inc(w_in, 16)
                if "alpha" in parts:
                    sp.wait_ge(al_done, CT)
                    sp.wait_ge(wk_done, 1)
                    load_x2(sp, x2d, 0, xn, r0_in)

            walk(sp, chunk)
            store_x2(NB * CH + 1, NB * CH * C * QC)

        @block.tensor
        def _(pe):
            pe.wait_ge(w1_in, 16)
            held = {k: None for k in range(5)}

            def take(bank):
                if held[bank]:
                    pe.wait_ge(*held[bank])

            def project(s, sl, half, bank):
                take(bank)
                for c in range(CT):
                    mm = pe.matmul(misc[bank][:, 0:256], w1s[:, c, :], xn[:, c, ds(sl * 512 + half * 256, 256)],
                                   start=c == 0, stop=c == CT - 1)
                mm.then_inc(f_filled, 1)
                held[bank] = (f_copied, s * 2 + (half + 1))

            def scan(T, i, q0, bank, a, bq):
                take(bank)
                mc = i // QT
                pe.matmul(banks[bank][:, 0:SC], a[0:KE, ds(q0 + (i % QT) * 128, 128)],
                          bq[0:KE, mc * SC:(mc + 1) * SC], start=True, stop=True).then_inc(scan_filled, 1)
                held[bank] = (scan_reduced, T * SCN + i + 1)

            def shift(T, bank):
                pe.wait_ge(ms_done, T + 1)
                take(bank)
                pe.transpose(banks[bank][0:3 * QT, 0:64].bitcast(BF16), ms[:, :], idb[:, :]).then_inc(m_filled, 1)
                held[bank] = (m_copied, T + 1)

            def back(t, bank):
                pe.wait_ge(evac_done, t * 2 + 2)
                take(bank)
                for c in range(CT):
                    for i in range(QT):
                        mm = pe.transpose(misc[bank][:, c * QC + i * 128:c * QC + (i + 1) * 128],
                                          x2t[:, i, c * 128:(c + 1) * 128], idf[:, :])
                mm.then_inc(back_filled, 1)
                held[bank] = (back_copied, t + 1)

            def energy(g, c0):
                for k in range(GM):
                    m = g * GM + k
                    mm = pe.matmul(pe2[g % 2][:, k * QC:(k + 1) * QC], A[0:KS, m * 128:(m + 1) * 128],
                                   Bq[0:KS, ds(c0, QC)], start=True, stop=True)
                mm.then_inc(e_done, 1)

            def attend(t, g, between):
                for i in range(QT):
                    for k in range(GM):
                        between(i * GM + k)
                        if i == 0 and k == 0:
                            pe.wait_ge(pl_done, t * G + (g + 1))
                        if g == 0 and k == 0:
                            pe.wait_ge(evac_done, t * 2 + (i + 1))
                        m = g * GM + k
                        first, last = g == 0 and k == 0, g == G - 1 and k == GM - 1
                        ph = Ph[:, g % RP, k, i * 128:(i + 1) * 128]
                        pl = Pl[:, g % RP, k, i * 128:(i + 1) * 128]
                        pe.matmul(acc[i][:, 0:C + 2], ph, xh[:, m, :], start=first, stop=False)
                        pe.matmul(acc[i][:, 0:C], ph, xl[:, m, :], start=False, stop=False)
                        mm = pe.matmul(acc[i][:, 0:C + 2], pl, xh[:, m, :], start=False, stop=last)
                        if last and i < QT - 1:
                            mm.then_inc(acc_done, 1)
                        if k == GM - 1 and i == QT - 1:
                            mm.then_inc(av_done, 1)

            pe.wait_ge(fill_done, 1)
            for s in range(SL + 1):
                if s < SL:
                    pe.wait_ge(x_in[s], 16)
                    if s >= 2:
                        pe.wait_ge(f_copied, 2 * (s - 1))
                    for c in range(CT):
                        mm = pe.matmul(pe2[s % 2][:, 0:512], w1s[:, c, :], xn[:, c, s * 512:(s + 1) * 512],
                                       start=c == 0, stop=c == CT - 1)
                    mm.then_inc(f_filled, 2)
                if s > 0:
                    pe.wait_ge(ab_done, 4 * s + 1)
                    for i in range((s - 1) * QT, s * QT):
                        scan(0, i, 0, i % 4, An, Bn)
            for i in range(SCN):
                if i == 2:
                    pe.wait_ge(const_in, 32)
                    pe.wait_ge(idb_done, 1)
                    pe.wait_ge(f_copied, 2 * SL)
                    shift(0, SHIFT0)
                scan(1, i, QC, 2 + i % 2, An, Bn)
                if i == SCN // 2 + 1:
                    pe.wait_ge(border_done, 2)
                    pe.wait_ge(m_stored, 16)
                    energy(0, 0)
            energy(1, 0)

            def chunk(b, j, parts):
                t = b * CH + j
                items = items_of(parts)
                if "last" in parts:
                    held[0], held[1] = (back_copied, t), (m_copied, t + 1)
                else:
                    for k in range(2):
                        held[k] = (scan_reduced, (t + 1) * SCN + (SCN - 1 + k))
                for g in range(G):
                    if "last" not in parts or g < G - 2:
                        pe.wait_ge(ph_done, t * G + (g + 1))
                        if g < G - 2:
                            energy(g + 2, j * QC)
                        else:
                            if g == G - 2:
                                pe.wait_ge(m_stored, (t + 2) * 16)
                            if "border" in parts and g == G - 2:
                                pe.wait_ge(border_done, (b + 2) * 2)
                            energy(g + 2 - G, 0 if "border" in parts else (j + 1) * QC)

                    def between(slot):
                        for at, kind, k, bank in items[g]:
                            if at != slot:
                                continue
                            if kind == "shift":
                                shift(t + 1, bank)
                            elif kind == "back":
                                back(t, bank)
                            elif kind == "project":
                                for q in range(XQ if k == 0 else 0):
                                    pe.wait_ge(x_in[q], (b + 2) * 16)
                                project((b + 1) * SL + (j - 3), j - 3, k, bank)
                            elif "scan_next" in parts:
                                scan(t + 2, 2 * g + k, (j - (CH - 2)) * QC, bank, An, Bn)
                            else:
                                scan(t + 2, 2 * g + k, (j + 2) * QC, bank, A, Bq)
                        if slot == 0 and "fresh" in parts:
                            pe.wait_ge(xl_done, b * G + (g + 1))
                    attend(t, g, between)

            walk(pe, chunk)
            held[0], held[1] = (back_copied, NB * CH), None
            back(NB * CH, 0)

        @block.scalar
        def _(act):
            def exps(q, g):
                act.wait_ge(e_done, q + 1)
                if not (isinstance(q, int) and q < 2):
                    act.wait_ge(pl_done, q - 1)
                nc.scalar.activation(P[:, g % 2, :], pe2[g % 2][:], ACT.Exp)
                if not (isinstance(q, int) and q < 2):
                    act.wait_ge(av_done, q - 1)
                nc.scalar.activation(Ph[:, g % RP, :, :].rearrange("p k n -> p (k n)"), pe2[g % 2][:],
                                     ACT.Exp).then_inc(ph_done, 1)

            def project(s, half, bank):
                n = slice(half * 256, (half + 1) * 256)
                act.wait_ge(f_filled, s * 2 + (half + 1))
                if not (isinstance(s, int) and s == 0):
                    act.wait_ge(ab_done, s * 4 + (2 * half - 1))
                nc.scalar.activation(Fp[0:KS, n], misc[bank][0:KS, 0:256], ACT.Identity, bias=col[0:KS, 0:1])
                nc.scalar.activation(f1[0:KS, n], misc[bank][0:KS, 0:256], ACT.Identity,
                                     bias=col[0:KS, 0:1]).then_inc(f_copied, 1)

            def upper(b, g, used):
                uses = len(range(g % XB, G, XB))
                act.wait_ge(xt_in[g % XB], b * (16 * uses) + (g // XB + 1) * 16)
                if used is not None:
                    act.wait_ge(xs_done, used[0])
                    act.wait_ge(av_done, used[1])
                nc.scalar.copy(xh[:, g * GM:(g + 1) * GM, 0:C],
                               landed[g % XB].rearrange("p (k c) -> p k c", k=GM)).then_inc(xh_done, 1)

            def back(t, bank):
                act.wait_ge(back_filled, t + 1)
                act.wait_ge(x2_stored, t * 16 + 1)
                nc.scalar.copy(x2s[:, :, :].rearrange("p c n -> p (c n)"), misc[bank][:]).then_inc(back_copied, 1)

            act.wait_ge(const_in, 32)
            nc.scalar.activation(warm[:], col[:, 0:1], ACT.Exp).then_inc(warm_done, 1)
            for s in range(SL + 1):
                if s < SL:
                    act.wait_ge(f_filled, 2 * s + 2)
                    if s > 0:
                        act.wait_ge(split_step, 6 * s)
                        act.wait_ge(first_f2, s)
                    bank = pe2[s % 2][0:KS, 0:512]
                    nc.scalar.activation(Fp[0:KS, :], bank, ACT.Identity, bias=col[0:KS, 0:1])
                    nc.scalar.activation(f1[0:KS, :], bank, ACT.Identity, bias=col[0:KS, 0:1]).then_inc(f_copied, 2)
                if s > 0:
                    n = slice((s - 1) * 512, s * 512)
                    act.wait_ge(ab_done, 4 * s + 1)
                    last = nc.scalar.copy(A[0:KS, n], An[0:KS, n])
                    if s == SL:
                        last.then_inc(border_done, 1)
                    last = nc.scalar.copy(Bq[0:KS, n], Bn[0:KS, n])
                    if s == SL:
                        last.then_inc(border_done, 1)
                if s >= 2:
                    upper(0, s - 2, None)
            for k in range(2):
                exps(k, k)

            def chunk(b, j, parts):
                t = b * CH + j
                items = items_of(parts)
                for g in range(G):
                    if "last" not in parts or g < G - 2:
                        exps(t * G + (g + 2), (g + 2) % G)
                    for _, kind, k, bank in items[g]:
                        if kind == "back":
                            back(t, bank)
                        elif kind == "project":
                            project((b + 1) * SL + (j - 3), k, bank)
                    if "border" in parts and g > 0:
                        upper(b + 1, g - 1, (t + 2, t * G + (g + 2)))
                    if "fresh" in parts and g == 0:
                        upper(b, G - 1, (t + 1, t * G + 2))
                    if "weights" in parts and g in (0, 2):
                        act.wait_ge(w_in, 16 * CT)
                        c = g // 2
                        nc.scalar.activation(sw[c].rearrange("p t o -> p (t o)"), xn[:, c, 0:TAPS * C],
                                             ACT.Sign).then_inc(w_signed, 1)
                    if "last" in parts and g < 2 * CT:
                        u, c = divmod(g, CT)
                        act.wait_ge(pad_zero, 2)
                        sign_unit(nc, act, 0, u, xn, r0_in, 32, pads, signed, (c,))

            walk(act, chunk)
            back(NB * CH, 0)

        @block.vector
        def _(dve):
            dve.wait_ge(const_in, 32)
            nc.vector.memset(x2t[:], 0.0).then_inc(evac_done, 2)
            nc.vector.memset(f2[:], 0.0).then_inc(ab_done, 1)
            nc.vector.tensor_copy(idb[:], idf[:]).then_inc(idb_done, 1)

            def split_parts(s, half):
                n = slice(half * 256, (half + 1) * 256)
                dve.wait_ge(f_copied, s * 2 + (half + 1))
                dve.wait_ge(ab_done, s * 4 + (2 * half + 1))
                nc.vector.scalar_tensor_tensor(f2[0:KS, n], f1[0:KS, n], -1.0, Fp[0:KS, n],
                                               ALU.mult, ALU.add).then_inc(split_step, 1)
                nc.vector.scalar_tensor_tensor(ta[0:KS, n], f1[0:KS, n], col[0:KS, 1:2], Fp[0:KS, n],
                                               ALU.mult, ALU.add).then_inc(split_step, 1)
                nc.vector.scalar_tensor_tensor(tb[0:KS, n], f1[0:KS, n], col[0:KS, 3:4], Fp[0:KS, n],
                                               ALU.mult, ALU.add).then_inc(split_step, 1)

            def split_rows(s, sl, half):
                n = slice(half * 256, (half + 1) * 256)
                dve.wait_ge(split_step, s * 6 + (3 * half + 3))
                nc.vector.scalar_tensor_tensor(An[0:KS, ds(sl * 512 + half * 256, 256)], f2[0:KS, n],
                                               col[0:KS, 2:3], ta[0:KS, n], ALU.mult, ALU.add).then_inc(ab_done, 1)
                nc.vector.scalar_tensor_tensor(Bn[0:KS, ds(sl * 512 + half * 256, 256)], f2[0:KS, n],
                                               col[0:KS, 4:5], tb[0:KS, n], ALU.mult, ALU.add).then_inc(ab_done, 1)

            def scan(T, i, bank):
                dve.wait_ge(scan_filled, T * SCN + (i + 1))
                if i == 0 and not (isinstance(T, int) and T == 0):
                    dve.wait_ge(neg_done, T)
                nc.vector.tensor_reduce(pm[:, i:i + 1], banks[bank][:, 0:SC], AX.X, ALU.max).then_inc(scan_reduced, 1)
                if i == SCN - 1:
                    dve.wait_ge(scan_reduced, T * SCN + SCN)
                    dve.wait_ge(ms_done, T)
                    nc.vector.tensor_reduce(negm[:], pm[:].rearrange("p (k i) -> p i k", i=QT), AX.X, ALU.max,
                                            negate=True).then_inc(neg_done, 1)

            def shift(T, bank):
                dve.wait_ge(m_filled, T + 1)
                dve.wait_ge(m_stored, T * 16)
                nc.vector.tensor_copy(mrow[:, :], banks[bank][0:3 * QT, 0:64].bitcast(BF16)).then_inc(m_copied, 1)

            def border(b, t, g):
                half, groups, cols = (G - 2) * GM * 64, (G - 2) * GM * 128, N - QC
                mid = cols // 2
                if g == 1:
                    dve.wait_ge(ab_done, (b + 1) * (4 * SL) + 1)
                    dve.wait_ge(e_done, t * G + 1)
                    nc.vector.tensor_copy(Bq[0:KS, QC:mid], Bn[0:KS, QC:mid])
                if g == 2:
                    dve.wait_ge(e_done, t * G + (G - 2) // 2)
                    nc.vector.tensor_copy(A[0:KS, 0:half], An[0:KS, 0:half])
                if g == 3:
                    nc.vector.tensor_copy(Bq[0:KS, mid:cols], Bn[0:KS, mid:cols])
                if g == 4:
                    dve.wait_ge(e_done, t * G + (G - 2))
                    nc.vector.tensor_copy(A[0:KS, half:groups], An[0:KS, half:groups])
                    dve.wait_ge(m_stored, (t + 2) * 16)
                    nc.vector.tensor_copy(Bq[0:KS, 0:QC], Bn[0:KS, 0:QC])
                if g == 5:
                    dve.wait_ge(e_done, (t + 1) * G)
                    nc.vector.tensor_copy(A[0:KS, groups:N], An[0:KS, groups:N]).then_inc(border_done, 1)
                    nc.vector.tensor_copy(Bq[0:KS, cols:N], Bn[0:KS, cols:N]).then_inc(border_done, 1)

            def lower(q, g):
                dve.wait_ge(ph_done, q + 1)
                nc.vector.tensor_tensor(Pl[:, g % RP, :, :].rearrange("p k n -> p (k n)"), P[:, g % 2, :],
                                        Ph[:, g % RP, :, :].rearrange("p k n -> p (k n)").bitcast(F32),
                                        ALU.subtract).then_inc(pl_done, 1)

            def evacuate(t, i):
                if i < QT - 1:
                    dve.wait_ge(acc_done, t + 1)
                else:
                    dve.wait_ge(av_done, t * G + (G + 2))
                nc.vector.reciprocal(rd[:, i:i + 1], acc[i][:, C:C + 1]).then_inc(rd_done, 1)
                dve.wait_ge(rd_done, t * 2 + (i + 1))
                dve.wait_ge(xs_done, t + 2)
                dve.wait_ge(back_filled, t + 1)
                nc.vector.scalar_tensor_tensor(x2t[:, i, :], acc[i][:, 0:C], rd[:, i:i + 1], xs[:, i, :],
                                               ALU.mult, ALU.add).then_inc(evac_done, 1)

            def make_weights(c, part):
                rows = [sw[c][:, 3 * k:3 * k + 3, :] for k in range(3)]
                if part == 0:
                    dve.wait_ge(w_signed, c + 1)
                    nc.vector.tensor_copy(wk[:, c, 0, :, :], rows[0])
                    nc.vector.tensor_copy(wk[:, c, 3, :, :], rows[2])
                    nc.vector.tensor_tensor(wk[:, c, 1, :, :], rows[0], rows[2], ALU.add).then_inc(outer_done, 1)
                if part == 1:
                    dve.wait_ge(outer_done, c + 1)
                    nc.vector.tensor_tensor(wk[:, c, 2, :, :], wk[:, c, 1, :, :], rows[1],
                                            ALU.subtract).then_inc(inner_done, 1)
                if part == 2:
                    dve.wait_ge(inner_done, c + 1)
                    last = nc.vector.tensor_tensor(wk[:, c, 1, :, :], wk[:, c, 1, :, :], rows[1], ALU.add)
                    if c == CT - 1:
                        last.then_inc(wk_done, 1)

            for s in range(SL):
                dve.wait_ge(f_copied, 2 * s + 2)
                if s > 0:
                    dve.wait_ge(ab_done, 4 * s + 1)
                nc.vector.scalar_tensor_tensor(ta[0:KS, :], f1[0:KS, :], col[0:KS, 1:2], Fp[0:KS, :],
                                               ALU.mult, ALU.add).then_inc(split_step, 3)
                nc.vector.scalar_tensor_tensor(tb[0:KS, :], f1[0:KS, :], col[0:KS, 3:4], Fp[0:KS, :],
                                               ALU.mult, ALU.add).then_inc(split_step, 3)
                dve.wait_ge(first_f2, s + 1)
                dve.wait_ge(split_step, 6 * s + 6)
                n = slice(s * 512, (s + 1) * 512)
                nc.vector.scalar_tensor_tensor(An[0:KS, n], f2[0:KS, :], col[0:KS, 2:3],
                                               ta[0:KS, :], ALU.mult, ALU.add).then_inc(ab_done, 2)
                nc.vector.scalar_tensor_tensor(Bn[0:KS, n], f2[0:KS, :], col[0:KS, 4:5],
                                               tb[0:KS, :], ALU.mult, ALU.add).then_inc(ab_done, 2)
                if s > 0:
                    for i in range((s - 1) * QT, s * QT):
                        scan(0, i, i % 4)
            for i in range((SL - 1) * QT, SL * QT):
                scan(0, i, i % 4)
            for i in range(SCN):
                if i == 2:
                    shift(0, SHIFT0)
                scan(1, i, 2 + i % 2)
            lower(0, 0)

            def chunk(b, j, parts):
                t = b * CH + j
                items = items_of(parts)
                for g in range(G):
                    for _, kind, k, bank in items[g]:
                        if kind == "scan":
                            scan(t + 2, 2 * g + k, bank)
                    if "border" in parts and g == 5:
                        border(b + 1, t, g)
                    if "last" not in parts or g < G - 1:
                        lower(t * G + (g + 1), (g + 1) % G)
                    for _, kind, k, bank in items[g]:
                        if kind == "shift":
                            shift(t + 1, bank)
                    if "border" in parts and g < 5:
                        border(b + 1, t, g)
                    if "project" in parts and g - 1 in PROJECT_AT:
                        split_parts((b + 1) * SL + (j - 3), PROJECT_AT.index(g - 1))
                    if "project" in parts and g - 2 in PROJECT_AT:
                        split_rows((b + 1) * SL + (j - 3), j - 3, PROJECT_AT.index(g - 2))
                    if g == G - 1:
                        for i in range(QT):
                            evacuate(t, i)
                    if "weights" in parts and g >= G - 3 * CT:
                        make_weights(*divmod(g - (G - 3 * CT), 3))
                    if "alpha" in parts and g in (1, 3):
                        dve.wait_ge(w_in, 16 * 2 * CT)
                        c = g // 3
                        nc.vector.tensor_reduce(al[:, c:c + 1], xn[:, c, 0:TAPS * C], AX.X, ALU.add,
                                                apply_absolute_value=True).then_inc(al_done, 1)

            walk(dve, chunk)

        @block.gpsimd
        def _(pool):
            nc.gpsimd.memset(xh[:, :, C:C + 2].bitcast(F32), DEN).then_inc(fill_done, 1)
            pool.wait_ge(fill_done, 1)
            nc.gpsimd.memset(mr[:], 0.0).then_inc(av_done, 2)
            nc.gpsimd.memset(xs[:], 0.0).then_inc(xs_done, 1)
            nc.gpsimd.memset(x2s[:], 0.0).then_inc(x2_stored, 1)

            pool.wait_ge(av_done, 2)

            def parts_of_max(T):
                pool.wait_ge(neg_done, T + 1)
                pool.wait_ge(m_filled, T)
                nc.gpsimd.tensor_tensor(ms[:, 0:QT], negm[:], mr[:, 1, :], ALU.add).then_inc(ms_step, 1)
                pool.wait_ge(ms_step, T * 3 + 1)
                nc.gpsimd.tensor_tensor(mr[:, 0, :], negm[:], ms[:, 0:QT], ALU.subtract).then_inc(ms_step, 1)
                pool.wait_ge(ms_step, T * 3 + 2)
                nc.gpsimd.tensor_tensor(ms[:, QT:2 * QT], mr[:, 0, :], mr[:, 1, :], ALU.add).then_inc(ms_step, 1)
                pool.wait_ge(ms_step, T * 3 + 3)
                nc.gpsimd.tensor_tensor(ms[:, 2 * QT:3 * QT], mr[:, 0, :], ms[:, QT:2 * QT],
                                        ALU.subtract).then_inc(ms_done, 1)

            def lower_x(b, g):
                pool.wait_ge(xh_done, b * G + (g + 1))
                k = slice(g * GM, (g + 1) * GM)
                nc.gpsimd.tensor_tensor(xl[:, k, :], landed[g % XB].rearrange("p (k c) -> p k c", k=GM),
                                        xh[:, k, 0:C].bitcast(F32), ALU.subtract).then_inc(xl_done, 1)

            for s in range(SL):
                pool.wait_ge(f_copied, 2 * s + 2)
                pool.wait_ge(ab_done, 4 * s + 1)
                nc.gpsimd.tensor_tensor(f2[0:KS, :], Fp[0:KS, :], f1[0:KS, :], ALU.subtract).then_inc(first_f2, 1)
                if s >= 3:
                    lower_x(0, s - 3)
            parts_of_max(0)
            for g in range(SL - 3, G - 1):
                lower_x(0, g)

            def chunk(b, j, parts):
                t = b * CH + j
                if "last" not in parts:
                    parts_of_max(t + 1)
                pool.wait_ge(evac_done, t * 2 + 2)
                if "fresh" in parts:
                    pool.wait_ge(xl_done, b * G + 1)
                else:
                    pool.wait_ge(xl_done, (b + 1) * G)
                nc.gpsimd.tensor_tensor(xs[:], xh[:, ds(j * QT, QT), 0:C].bitcast(F32),
                                        xl[:, ds(j * QT, QT), :].bitcast(F32), ALU.add).then_inc(xs_done, 1)
                if "border" in parts:
                    for g in range(G - 1):
                        lower_x(b + 1, g)
                if "fresh" in parts:
                    lower_x(b, G - 1)
                if "alpha" in parts:
                    for k in range(2):
                        nc.gpsimd.memset((fw, tab)[k][:], 0.0).then_inc(pad_zero, 1)
                if "last" in parts:
                    for u in range(2):
                        pool.wait_ge(signed, CT * (u + 1))
                        transform_unit(nc, pads[u], V[u], v_done)

            walk(pool, chunk)


def convolution(nc, gb, x2d, out, shared):
    SLOT = (0, 1, 2, 0)
    LAST = (1, 2, 3, 0)
    PIECE = UR * W
    xn, An, Bn, fw, tab, wk, x2s, al, sems = shared
    w_in, w_signed, wk_done, al_done, r0_in, pad_zero, signed, v_done, x2_stored = sems
    pads = [pad_view(fw), pad_view(tab)]
    V = [v_view(An), v_view(Bn)]
    wk_flat = wk[:, :, :, :, :].rearrange("p c k x o -> p (c k x o)")
    homes = [fw[:, 0:PIECE], tab[:, 0:PIECE]] + [
        t[:, m * 2 * PIECE:(m + 1) * 2 * PIECE].bitcast(F32) for t in (An, Bn, wk_flat) for m in range(2)]
    with ExitStack() as ctx:
        def sb(name, shape, dt):
            return ctx.enter_context(nc.sbuf_tensor(name, shape, dt))

        def sem(name):
            return ctx.enter_context(nc.semaphore(name))

        xr = [xn, sb("xr1", [128, CT, N], F32), sb("xr2", [128, CT, N], F32)]
        Y = sb("Y", [128, CT, NB * N], I16)
        m1 = sb("m1", [128, CT, UP * W], I16)
        plus = sb("plus", [128, UP * W], I16)
        minus = sb("minus", [128, UP * W], I16)
        none = sb("none", [128, CT, 1, PW], BF16)
        g2 = sb("g2", [128, 4], F32)
        st = sb("st", [128, CT, NB * UN * 2, 6], F32)
        mv = sb("mv", [128, CT, 2], F32)
        sm = sb("sm", [128, 12, CT], F32)
        eps = sb("eps", [128, 1], F32)
        pm = [[ctx.enter_context(nc.psum_tensor(f"pm{o}_{k}", [128, UP * W], F32)) for k in range(VK)]
              for o in range(CT)]

        g_in = sem("g_in")
        r_in = [r0_in] + [[sem(f"r_in{slot}_{k}") for k in range(UN)] for slot in (1, 2)]
        m_filled = sem("conv_filled")
        m1_done = sem("m1_done")
        half_done = sem("half_done")
        y_done = sem("y_done")
        edge_done = sem("edge_done")
        none_done = sem("none_done")
        stats_done = sem("stats_done")
        step = sem("step")
        aggregated = sem("aggregated")
        root_in = sem("root_in")
        root_done = sem("root_done")
        coef_done = sem("coef_done")
        home_in = sem("home_in")
        shift_added = sem("shift_added")
        r_done = sem("r_done")
        stored = sem("stored")
        block = ctx.enter_context(nc.Block())
        SM = (lambda k: sm[:, k, :])

        def pieces():
            for b in LAST:
                for c in range(CT):
                    for k in range(UN):
                        yield b, c, k, (xr[SLOT[b]][:, c, k * PIECE:(k + 1) * PIECE] if b else homes[c * UN + k])

        ORDER = (1, 2, 0, 3)

        @block.sync
        def _(sp):
            sp.dma_start(g2[:], gb).then_inc(g_in, 16)
            load_x2(sp, x2d, 1, xr[1], r_in[1])
            load_x2(sp, x2d, 2, xr[2], r_in[2])
            sp.wait_ge(signed, CT * UN)
            sp.wait_ge(x2_stored, 16 * (NB * CH + 1) + 1)
            load_x2(sp, x2d, 3, xr[0], r_in[0])
            view = x2d.rearrange("(t p n) -> t p n", p=128, n=CT * QC)
            per = CH // UN
            for h, home in enumerate(homes):
                c, k = divmod(h, UN)
                if h == 0:
                    sp.wait_ge(v_done, NB * UN)
                if h == 2:
                    sp.wait_ge(m_filled, (NB * UN - 1) * CT * VK)
                if h == 4:
                    sp.wait_ge(m_filled, NB * UN * CT * VK)
                sp.dma_start(home.rearrange("p (j n) -> p j n", n=QC),
                             view[1 + k * per:1 + (k + 1) * per, :, c * QC:(c + 1) * QC].rearrange("j p n -> p j n")
                             ).then_inc(home_in, 16)
            for n, (b, c, k, r) in enumerate(pieces()):
                sp.wait_ge(r_done, n + 1)
                sp.dma_start(out[b, c * 128:(c + 1) * 128, k * PIECE:(k + 1) * PIECE], r).then_inc(stored, 16)
            n = NB * CT * UN
            sp.wait_ge(stored, 16 * n)

        @block.gpsimd
        def _(pool):
            nc.gpsimd.memset(none[:], 0.0).then_inc(none_done, 1)
            pool.wait_ge(none_done, 1)

            def unit(U, u, edges):
                pool.wait_ge(m_filled, (U - 1) * (VK * CT))
                if u == 0:
                    nc.gpsimd.tensor_tensor(pads[0][:, :, 0:1, :], none[:], none[:], ALU.add).then_inc(edge_done, 1)
                    pool.wait_ge(edge_done, edges)
                if u == UN - 1:
                    nc.gpsimd.tensor_tensor(pads[1][:, :, UR + 1:UR + 2, :], none[:], none[:],
                                            ALU.add).then_inc(edge_done, 1)
                    pool.wait_ge(edge_done, edges)
                pool.wait_ge(signed, U * CT + CT)
                transform_unit(nc, pads[u % 2], V[u % 2], v_done)

            unit(2, 2, 0)
            unit(3, 3, 1)
            with pool.Fori(1, NB) as b:
                for u in range(UN):
                    unit(b * UN + u, u, b * 2 + (0 if u == 0 else 1))

        @block.scalar
        def _(act):
            for U in range(NB * UN):
                if U + 2 < NB * UN:
                    b, u = divmod(U + 2, UN)
                    act.wait_ge(v_done, U + 1)
                    sign_unit(nc, act, b, u, xr[SLOT[b]], r_in[SLOT[b]], 64 if b == 3 else 32, pads, signed)
                for o in range(CT):
                    n = U * CT + o
                    act.wait_ge(m_filled, VK * n + 1)
                    nc.scalar.copy(m1[:, o, :], pm[o][1][:]).then_inc(m1_done, 1)
            act.wait_ge(root_in, 1)
            nc.scalar.activation(SM(3), SM(2), ACT.Sqrt, bias=eps[:]).then_inc(root_done, 1)
            act.wait_ge(coef_done, 2)
            for b, c, k, r in pieces():
                if b:
                    act.wait_ge(r_in[SLOT[b]][k], 64 if b == 3 else 32)
                else:
                    act.wait_ge(home_in, 16 * len(homes))
                nc.scalar.activation(r, r, ACT.Identity, bias=sm[:, 9, c:c + 1]).then_inc(shift_added, 1)

        @block.tensor
        def _(pe):
            pe.wait_ge(wk_done, 1)
            with pe.Fori(0, NB * UN // 2) as h:
                for u in range(2):
                    pe.wait_ge(v_done, h * 2 + (u + 1))
                    for o in range(CT):
                        pe.wait_ge(y_done, h * (2 * CT) + (u * CT + o + 1))
                        for k in ORDER:
                            for c in range(CT):
                                for dx in range(3):
                                    mm = pe.matmul(pm[o][k][:], wk[:, c, k, dx, o * 128:(o + 1) * 128],
                                                   V[u][:, k, c, :, dx:dx + W],
                                                   start=c == 0 and dx == 0, stop=c == CT - 1 and dx == 2)
                            mm.then_inc(m_filled, 1)

        @block.vector
        def _(dve):
            nc.vector.memset(eps[:], EPS).then_inc(y_done, 2)
            dve.wait_ge(al_done, CT)
            dve.wait_ge(g_in, 16)
            count = [0]

            def then(ins):
                count[0] += 1
                ins.then_inc(step, 1)
                dve.wait_ge(step, count[0])

            then(nc.vector.tensor_scalar(SM(0), al[:], 1.0 / (C * TAPS), None, ALU.mult))
            then(nc.vector.tensor_tensor(SM(1), SM(0), SM(0), ALU.mult))
            then(nc.vector.tensor_tensor(SM(5), SM(0), g2[:, 0:2], ALU.mult))

            with dve.Fori(0, NB * UN // 2) as h:
                for u in range(2):
                    for o in range(CT):
                        n = u * CT + o
                        y = Y[:, o, ds(h * (2 * PIECE) + u * PIECE, PIECE)]
                        rows = y.rearrange("p (r two w) -> p r two w", two=2, w=W)
                        dve.wait_ge(m1_done, h * (2 * CT) + (n + 1))
                        dve.wait_ge(m_filled, h * (2 * CT * VK) + (n * VK + 2))
                        nc.vector.tensor_tensor(plus[:], pm[o][2][:], m1[:, o, :], ALU.add).then_inc(half_done, 1)
                        nc.vector.tensor_tensor(minus[:], m1[:, o, :], pm[o][2][:],
                                                ALU.subtract).then_inc(half_done, 1)
                        dve.wait_ge(half_done, h * (4 * CT) + (2 * n + 2))
                        dve.wait_ge(m_filled, h * (2 * CT * VK) + (n * VK + 3))
                        nc.vector.scalar_tensor_tensor(
                            rows[:, :, 0, :], plus[:].rearrange("p (r w) -> p r w", w=W), 0.5,
                            pm[o][0][:].rearrange("p (r w) -> p r w", w=W), ALU.mult, ALU.add)
                        dve.wait_ge(m_filled, h * (2 * CT * VK) + (n * VK + 4))
                        nc.vector.scalar_tensor_tensor(
                            rows[:, :, 1, :], minus[:].rearrange("p (r w) -> p r w", w=W), 0.5,
                            pm[o][3][:].rearrange("p (r w) -> p r w", w=W), ALU.mult, ALU.subtract
                        ).then_inc(y_done, 1)
                        dve.wait_ge(y_done, h * (2 * CT) + (n + 3))
                        for k in range(2):
                            nc.vector.bn_stats(st[:, o, ds(h * 4 + (u * 2 + k), 1), :].rearrange("p a s -> p (a s)"),
                                               Y[:, o, ds(h * (2 * PIECE) + (u * PIECE + k * 512), 512)]
                                               ).then_inc(stats_done, 1)
            dve.wait_ge(stats_done, NB * UN * CT * 2)
            for c in range(CT):
                nc.vector.bn_aggr(mv[:, c, :], st[:, c, :, :].rearrange("p a s -> p (a s)")).then_inc(aggregated, 1)
            dve.wait_ge(aggregated, CT)
            nc.vector.tensor_tensor(SM(2), SM(1), mv[:, :, 1], ALU.mult).then_inc(root_in, 1)
            dve.wait_ge(root_done, 1)
            then(nc.vector.reciprocal(SM(4), SM(3)))
            then(nc.vector.tensor_tensor(SM(7), SM(5), SM(4), ALU.mult))
            then(nc.vector.tensor_tensor(SM(8), SM(7), mv[:, :, 0], ALU.mult))
            nc.vector.tensor_tensor(SM(9), g2[:, 2:4], SM(8), ALU.subtract).then_inc(coef_done, 2)
            for n, (b, c, k, r) in enumerate(pieces()):
                dve.wait_ge(shift_added, n + 1)
                nc.vector.scalar_tensor_tensor(r, Y[:, c, b * N + k * PIECE:b * N + (k + 1) * PIECE],
                                               sm[:, 7, c:c + 1], r, ALU.mult, ALU.add).then_inc(r_done, 1)


def build(nc, x, xt, w1r, cols, ident, wn, wt, gb, x2d, out):
    with ExitStack() as ctx:
        def sb(name, shape, dt):
            return ctx.enter_context(nc.sbuf_tensor(name, shape, dt))

        def sem(name):
            return ctx.enter_context(nc.semaphore(name))

        xn = sb("xn", [128, CT, N], F32)
        An = sb("An", [128, VLEN], BF16)
        Bn = sb("Bn", [128, VLEN], BF16)
        fw = sb("fw", [128, PADLEN // 2], F32)
        tab = sb("tab", [128, PADLEN // 2], F32)
        wk = sb("wk", [128, CT, VK, 3, C], BF16)
        x2s = sb("x2s", [128, CT, QC], F32)
        al = sb("al", [128, CT], F32)
        sems = (sem("w_in"), sem("w_signed"), sem("wk_done"), sem("al_done"),
                [sem(f"r_in0_{k}") for k in range(UN)], sem("pad_zero"), sem("signed"), sem("v_done"),
                sem("x2_stored"))
        shared = (xn, An, Bn, fw, tab, wk, x2s, al, sems)
        attention(nc, x, xt, w1r, cols, ident, wn, wt, x2d, shared)
        convolution(nc, gb, x2d, out, shared)


def kernel(x, L0_conv_w1, L0_conv_b1, L1_conv_weights, L1_conv_gamma, L1_conv_beta):
    import concourse.bacc as bacc
    from concourse.bass_utils import run_bass_kernel_spmd as run

    f32 = np.float32
    w1, b1, w = (np.asarray(a) for a in (L0_conv_w1, L0_conv_b1, L1_conv_weights))
    w1r = np.zeros((C, 128), f32)
    cols = np.zeros((128, 8), f32)
    for r, (a, q) in enumerate(zip(SPLIT_A, SPLIT_B)):
        rows = slice(r * KF, (r + 1) * KF)
        w1r[:, rows] = w1.T
        cols[rows, 0] = b1
        for k, part in ((1, a), (3, q)):
            cols[rows, k] = -1.0 if part >= 2 else 0.0
            cols[rows, k + 1] = -1.0 if part >= 3 else 0.0
    cols[KE:KS, 0] = 1.0
    gb = np.concatenate([np.asarray(a).reshape(CT, 128).T for a in (L1_conv_gamma, L1_conv_beta)], axis=1)
    arrays = {
        "x": np.ascontiguousarray(np.asarray(x).reshape(-1)),
        "xt": np.ascontiguousarray(np.asarray(x).reshape(NB, C, G, GM, 128).transpose(0, 2, 4, 3, 1).reshape(-1)),
        "w1r": w1r, "cols": cols, "ident": np.eye(128, dtype=f32),
        "wn": np.ascontiguousarray(w.reshape(CT, 128, C * TAPS)),
        "wt": np.ascontiguousarray(w.reshape(C, CT, 128, TAPS).transpose(1, 2, 3, 0).reshape(CT, 128, TAPS * C)),
        "gb": np.ascontiguousarray(gb),
    }
    nc = bacc.Bacc("TRN2", target_bir_lowering=False, num_devices=1)
    args = [nc.dram_tensor(n, a.shape, F32, kind="ExternalInput").ap() for n, a in arrays.items()]
    args.append(nc.dram_tensor("x2", ((NB * CH + 1) * C * QC,), F32, kind="Internal").ap())
    args.append(nc.dram_tensor("out", (NB, C, N), F32, kind="ExternalOutput").ap())
    build(nc, *args)
    return run(nc, [arrays], core_ids=[0]).results[0]["out"].reshape(NB, C, H, W)
```
